# Optimizing a Trainium2 kernel written in Bass

```python
import numpy as np
import jax
import jax.numpy as jnp

def _softmax(x, axis=-1):
    return jax.nn.softmax(x, axis=axis)

def _gelu(x):
    return jax.nn.gelu(x, approximate=True)

def _silu(x):
    return jax.nn.silu(x)

def _sigmoid(x):
    return jax.nn.sigmoid(x)

def _layernorm(x, axis=-1, eps=1e-05):
    m = jnp.mean(x, axis=axis, keepdims=True)
    v = jnp.var(x, axis=axis, keepdims=True)
    return (x - m) / jnp.sqrt(v + eps)

def _scatter_add(tgt, idx, src, axis=0):
    return tgt.at[idx].add(src)

def _segment_sum(src, seg, n):
    return jax.ops.segment_sum(src, seg, n)
kernel_name = 'mk_xattn_ffn_d1_seqx_r8_f5868a'

def setup_inputs(seed: int=0):
    np.random.seed(seed)
    _w = jnp.asarray

    def _rec_inputs():
        import jax
        import jax.numpy as jnp
        _rk = jax.random.key(seed)
        x = -0.0002928 + 1 * jax.random.normal(jax.random.fold_in(_rk, 1), (4, 256, 128), jnp.float32)
        _lenS = 256 - jax.random.randint(jax.random.fold_in(_rk, 7), (4,), 0, max(1, 256 // 4) + 1, jnp.int32)
        _lenS2 = 256 - jax.random.randint(jax.random.fold_in(_rk, 8), (4,), 0, max(1, 256 // 4) + 1, jnp.int32)
        _ctx_1024P = jax.random.normal(jax.random.fold_in(_rk, 11), (4, 16, 128), jnp.float32)
        _ctx_1024c = jax.random.dirichlet(jax.random.fold_in(_rk, 511), 0.3 * jnp.ones((16,), jnp.float32), (4, 256))
        _ctx_1024t = jnp.einsum('bsk,bkd->bsd', _ctx_1024c, _ctx_1024P)
        _ctx_1024t = _ctx_1024t * jax.lax.rsqrt(jnp.mean(jnp.square(_ctx_1024t)) + 1e-12) * 0.953939
        ctx_1024 = -1.39393e-06 + 0.999914 * (_ctx_1024t + 0.3 * jax.random.normal(jax.random.fold_in(_rk, 611), (4, 256, 128), jnp.float32))
        _validS = jnp.arange(256)[None, :] < _lenS[:, None]
        _validS2 = jnp.arange(256)[None, :] < _lenS2[:, None]
        _causal = jnp.tril(jnp.ones((256, 256), dtype=bool))
        mask_BxSxS2_ik0 = jnp.where(jnp.broadcast_to(_validS2[:, None, :], (4, 256, 256)), 0, 1).astype(jnp.int32)
        return (x, ctx_1024, mask_BxSxS2_ik0)
    x, ctx_1024, mask_BxSxS2_ik0 = _rec_inputs()

    def _L0_xattn_setup():
        import jax, jax.numpy as jnp
        import numpy as np
        D_MODEL = 128
        NUM_HEADS = 16
        D_K = D_MODEL // NUM_HEADS
        BATCH = 2
        SEQ = 256
        key = jax.random.key(seed)
        k = jax.random.split(key, 8)
        query = jax.random.normal(k[0], (BATCH, SEQ, D_MODEL), dtype=jnp.float32)
        key_t = jax.random.normal(k[1], (BATCH, SEQ, D_MODEL), dtype=jnp.float32)
        value = jax.random.normal(k[2], (BATCH, SEQ, D_MODEL), dtype=jnp.float32)
        mask = jnp.broadcast_to(jnp.tril(jnp.ones((SEQ, SEQ), dtype=jnp.int32)), (BATCH, SEQ, SEQ))
        scale = 1.0 / np.sqrt(D_MODEL)
        w_q = jax.random.normal(k[3], (D_MODEL, D_MODEL), dtype=jnp.float32) * scale
        w_k = jax.random.normal(k[4], (D_MODEL, D_MODEL), dtype=jnp.float32) * scale
        w_v = jax.random.normal(k[5], (D_MODEL, D_MODEL), dtype=jnp.float32) * scale
        w_o = jax.random.normal(k[6], (D_MODEL, D_MODEL), dtype=jnp.float32) * scale
        b_o = jnp.zeros((D_MODEL,), dtype=jnp.float32)
        return {'query': query, 'key': key_t, 'value': value, 'mask': mask, 'w_q': w_q, 'w_k': w_k, 'w_v': w_v, 'w_o': w_o, 'b_o': b_o}
    _L0_xattn_all = _L0_xattn_setup()
    _L0_xattn_in = {k: v for k, v in _L0_xattn_all.items() if k in ('w_q', 'w_k', 'w_v', 'w_o', 'b_o')}
    del _L0_xattn_all

    def _L0_ffn_setup():
        import jax, jax.numpy as jnp
        import numpy as np
        N_EXPERTS = 32
        TOP_K = 8
        N_GROUP = 4
        TOPK_GROUP = 2
        ROUTED_SCALING = 2.5

        def _gate(x, gate_w, gate_bias):
            T, E = (x.shape[0], gate_w.shape[0])
            logits = jnp.einsum('th,eh->te', x, gate_w)
            scores = jax.nn.sigmoid(logits)
            scores_choice = scores + gate_bias[None, :]
            grp = scores_choice.reshape(T, N_GROUP, E // N_GROUP)
            top2, _ = jax.lax.top_k(grp, 2)
            group_scores = top2.sum(-1)
            _, grp_idx = jax.lax.top_k(group_scores, TOPK_GROUP)
            group_mask = jax.nn.one_hot(grp_idx, N_GROUP, dtype=scores.dtype).sum(1)
            expert_mask = jnp.repeat(group_mask, E // N_GROUP, axis=1)
            masked = jnp.where(expert_mask > 0, scores_choice, 0.0)
            _, topk_idx = jax.lax.top_k(masked, TOP_K)
            topk_w = jnp.take_along_axis(scores, topk_idx, axis=1)
            topk_w = topk_w / (topk_w.sum(-1, keepdims=True) + 1e-20)
            topk_w = topk_w * ROUTED_SCALING
            return (topk_idx, topk_w)

        def _mlp(x, wg, wu, wd):
            return jnp.einsum('...i,hi->...h', jax.nn.silu(jnp.einsum('...h,ih->...i', x, wg)) * jnp.einsum('...h,ih->...i', x, wu), wd)
        key = jax.random.key(seed)
        ks = jax.random.split(key, 9)
        B, S, H, I = (2, 64, 128, 64)
        w = 0.02
        return {'hidden_states': jax.random.normal(ks[0], (B, S, H), jnp.float32), 'gate_w': jax.random.normal(ks[1], (N_EXPERTS, H), jnp.float32) * w, 'gate_bias': jax.random.normal(ks[2], (N_EXPERTS,), jnp.float32) * w, 'expert_gate': jax.random.normal(ks[3], (N_EXPERTS, I, H), jnp.float32) * w, 'expert_up': jax.random.normal(ks[4], (N_EXPERTS, I, H), jnp.float32) * w, 'expert_down': jax.random.normal(ks[5], (N_EXPERTS, H, I), jnp.float32) * w, 'shared_gate': jax.random.normal(ks[6], (2 * I, H), jnp.float32) * w, 'shared_up': jax.random.normal(ks[7], (2 * I, H), jnp.float32) * w, 'shared_down': jax.random.normal(ks[8], (H, 2 * I), jnp.float32) * w}
    _L0_ffn_all = _L0_ffn_setup()
    _L0_ffn_in = {k: v for k, v in _L0_ffn_all.items() if k in ('gate_w', 'gate_bias', 'expert_gate', 'expert_up', 'expert_down', 'shared_gate', 'shared_up', 'shared_down')}
    del _L0_ffn_all
    return {'x': x, 'ctx_1024': ctx_1024, 'mask_BxSxS2_ik0': mask_BxSxS2_ik0, 'L0_xattn_w_q': _L0_xattn_in['w_q'], 'L0_xattn_w_k': _L0_xattn_in['w_k'], 'L0_xattn_w_v': _L0_xattn_in['w_v'], 'L0_xattn_w_o': _L0_xattn_in['w_o'], 'L0_xattn_b_o': _L0_xattn_in['b_o'], 'L0_ffn_gate_w': _L0_ffn_in['gate_w'], 'L0_ffn_gate_bias': _L0_ffn_in['gate_bias'], 'L0_ffn_expert_gate': _L0_ffn_in['expert_gate'], 'L0_ffn_expert_up': _L0_ffn_in['expert_up'], 'L0_ffn_expert_down': _L0_ffn_in['expert_down'], 'L0_ffn_shared_gate': _L0_ffn_in['shared_gate'], 'L0_ffn_shared_up': _L0_ffn_in['shared_up'], 'L0_ffn_shared_down': _L0_ffn_in['shared_down']}

def reference(x, ctx_1024, mask_BxSxS2_ik0, L0_xattn_w_q, L0_xattn_w_k, L0_xattn_w_v, L0_xattn_w_o, L0_xattn_b_o, L0_ffn_gate_w, L0_ffn_gate_bias, L0_ffn_expert_gate, L0_ffn_expert_up, L0_ffn_expert_down, L0_ffn_shared_gate, L0_ffn_shared_up, L0_ffn_shared_down):
    import jax
    import jax.numpy as jnp

    def _L0_xattn_ref(query, key, value, mask, w_q, w_k, w_v, w_o, b_o):
        import jax, jax.numpy as jnp
        import numpy as np
        D_MODEL = 128
        NUM_HEADS = 16
        D_K = D_MODEL // NUM_HEADS
        BATCH = 2
        SEQ = 256
        b, s, _ = query.shape

        def split_heads(x):
            return x.reshape(b, s, NUM_HEADS, D_K).transpose(0, 2, 1, 3)
        Q = split_heads(query @ w_q.T)
        K = split_heads(key @ w_k.T)
        V = split_heads(value @ w_v.T)
        scores = jnp.einsum('bhqd,bhkd->bhqk', Q, K) / jnp.sqrt(jnp.asarray(D_K, dtype=Q.dtype))
        scores = jnp.where(mask[:, None, :, :] == 0, -1000000000.0, scores)
        attn = jax.nn.softmax(scores, axis=-1)
        out = jnp.einsum('bhqk,bhkd->bhqd', attn, V)
        out = out.transpose(0, 2, 1, 3).reshape(b, s, D_MODEL)
        return out @ w_o.T + b_o

    def _L0_ffn_ref(hidden_states, gate_w, gate_bias, expert_gate, expert_up, expert_down, shared_gate, shared_up, shared_down):
        import jax, jax.numpy as jnp
        import numpy as np
        N_EXPERTS = 32
        TOP_K = 8
        N_GROUP = 4
        TOPK_GROUP = 2
        ROUTED_SCALING = 2.5

        def _gate(x, gate_w, gate_bias):
            T, E = (x.shape[0], gate_w.shape[0])
            logits = jnp.einsum('th,eh->te', x, gate_w)
            scores = jax.nn.sigmoid(logits)
            scores_choice = scores + gate_bias[None, :]
            grp = scores_choice.reshape(T, N_GROUP, E // N_GROUP)
            top2, _ = jax.lax.top_k(grp, 2)
            group_scores = top2.sum(-1)
            _, grp_idx = jax.lax.top_k(group_scores, TOPK_GROUP)
            group_mask = jax.nn.one_hot(grp_idx, N_GROUP, dtype=scores.dtype).sum(1)
            expert_mask = jnp.repeat(group_mask, E // N_GROUP, axis=1)
            masked = jnp.where(expert_mask > 0, scores_choice, 0.0)
            _, topk_idx = jax.lax.top_k(masked, TOP_K)
            topk_w = jnp.take_along_axis(scores, topk_idx, axis=1)
            topk_w = topk_w / (topk_w.sum(-1, keepdims=True) + 1e-20)
            topk_w = topk_w * ROUTED_SCALING
            return (topk_idx, topk_w)

        def _mlp(x, wg, wu, wd):
            return jnp.einsum('...i,hi->...h', jax.nn.silu(jnp.einsum('...h,ih->...i', x, wg)) * jnp.einsum('...h,ih->...i', x, wu), wd)
        orig_shape = hidden_states.shape
        H = orig_shape[-1]
        residuals = hidden_states
        x = hidden_states.reshape(-1, H)
        topk_idx, topk_w = _gate(x, gate_w, gate_bias)
        g = jnp.einsum('th,eih->eti', x, expert_gate)
        u = jnp.einsum('th,eih->eti', x, expert_up)
        outs = jnp.einsum('eti,ehi->eth', jax.nn.silu(g) * u, expert_down)
        outs_t = jnp.transpose(outs, (1, 0, 2))
        gathered = jnp.take_along_axis(outs_t, topk_idx[:, :, None], axis=1)
        final = (gathered * topk_w[:, :, None]).sum(1)
        shared = _mlp(residuals, shared_gate, shared_up, shared_down)
        return final.reshape(orig_shape) + shared
    x = x + _L0_xattn_ref(_layernorm(x, axis=-1), ctx_1024, ctx_1024, mask_BxSxS2_ik0, L0_xattn_w_q, L0_xattn_w_k, L0_xattn_w_v, L0_xattn_w_o, L0_xattn_b_o)
    x = x + _L0_ffn_ref(_layernorm(x, axis=-1), L0_ffn_gate_w, L0_ffn_gate_bias, L0_ffn_expert_gate, L0_ffn_expert_up, L0_ffn_expert_down, L0_ffn_shared_gate, L0_ffn_shared_up, L0_ffn_shared_down)
    return x

_drawn_inputs = setup_inputs


def setup_inputs(seed=0):
    import zlib

    import numpy as np

    out = dict(_drawn_inputs(seed))
    spreads = {'L0_xattn_b_o': (0.0, 0.1)}
    factors = {'L0_ffn_gate_w': 8.0,
     'L0_ffn_gate_bias': 8.0,
     'L0_ffn_expert_gate': 8.0,
     'L0_ffn_expert_up': 8.0,
     'L0_ffn_expert_down': 8.0,
     'L0_ffn_shared_gate': 8.0,
     'L0_ffn_shared_up': 8.0,
     'L0_ffn_shared_down': 8.0}
    for name, (base, spread) in spreads.items():
        noise = np.random.default_rng([zlib.crc32(name.encode()), seed]).standard_normal(out[name].shape)
        drawn = base * np.exp(spread * noise) if base else spread * noise
        out[name] = jnp.asarray(drawn.astype(out[name].dtype))
    for name, factor in factors.items():
        out[name] = (out[name] * factor).astype(out[name].dtype)
    return out
```

```python
from contextlib import ExitStack

import numpy as np

import concourse.bass as bass
from concourse import mybir

F32 = mybir.dt.float32
F32R = mybir.dt.float32r
BF16 = mybir.dt.bfloat16
I32 = mybir.dt.int32
ALU = mybir.AluOpType
ACT = mybir.ActivationFunctionType
AX = mybir.AxisListType

P = 128
B, S, D = 4, 256, 128
H, DK = 16, 8
T = B * S
NC = T // P
QC = S // P
PAIRS = H // 2
PARTS = 3
BLOCKS = 6
STACK = BLOCKS * DK
STACKM = STACK + PARTS
HALFP = P // 2
VW = 32
E, I = 32, 64
NG, GE = 4, 8
TOPK = 8
FF = E * I + 2 * I
NI = FF // P
HALF = T // 2
HC = HALF // P
MASKED = -float(2**30)
QSCALE = float(1.0 / np.sqrt(np.float32(DK)))
EPS = 1e-5
ROUTED_SCALING = 2.5
FILL = -3.0e38
TAKEN = 3.0e38
AHEAD = 12

SPANS = [(0, S), (S, S), (2 * S, 2 * S)]


def build(nc, x, ctxT, wqT, wkT, wvT, woT, bo, maskq, maskT, gwT, gbias, wgT, wuT, wdT,
          ident, identb, sel, ones, q_dram, k_dram, m_dram, outT):
    with ExitStack() as ctx:
        def sb(name, shape, dt):
            return ctx.enter_context(nc.sbuf_tensor(name, shape, dt))

        def psum(name, shape, dt=F32):
            return ctx.enter_context(nc.psum_tensor(name, shape, dt))

        def sem(name):
            return ctx.enter_context(nc.semaphore(name))

        x_sb = sb("x_sb", [P, NC, D], F32)
        xb_sb = x_sb
        bo_sb = sb("bo_sb", [P, D], F32)
        ctxT_sb = sb("ctxT_sb", [P, T], F32)
        wq_sb = sb("wq_sb", [P, P], F32)
        wk_sb = sb("wk_sb", [P, P], F32)
        wv_sb = sb("wv_sb", [P, P], F32)
        wo_sb = sb("wo_sb", [P, P], F32)
        id_sb = sb("id_sb", [P, P], F32)
        idb_sb = sb("idb_sb", [P, P], BF16)
        m_sb = sb("m_sb", [P, 2, B, QC, S], I32)
        mq_sb, mt_sb = m_sb[:, 0], m_sb[:, 1]
        biasq = sb("biasq", [P, B, QC, S], BF16)
        biast = sb("biast", [P, B, QC, S], BF16)
        top_bias = sb("top_bias", [P, NC], F32)
        any_key = sb("any_key", [P, NC], F32)
        stats = sb("stats", [P, NC, 6], F32)
        mean_var = sb("mean_var", [P, NC, 2], F32)
        vareps = sb("vareps", [P, NC], F32)
        rstd = sb("rstd", [P, NC], F32)
        rs = sb("rs", [P, NC], F32)
        minus_half = sb("minus_half", [P, NC], F32)
        xn = sb("xn", [P, NC, D], F32)
        xnT = sb("xnT", [P, T], F32)
        qp = sb("qp", [P, PARTS, T], BF16)
        kp = sb("kp", [P, PARTS, T], BF16)
        rest_q = sb("rest_q", [P, HALF], F32)
        rest_k = sb("rest_k", [P, HALF], F32)
        qs = sb("qs", [P, PAIRS, T], BF16)
        ks = sb("ks", [P, PAIRS, T], BF16)
        vs = sb("vs", [P, NC, H, VW], F32)
        top = sb("top", [P, B, QC, H], F32)
        top_rest = sb("top_rest", [P, QC, H], F32)
        ntop = sb("ntop", [P, QC, PARTS, H], BF16)
        ntopT = sb("ntopT", [PARTS * H, 2, S], BF16)
        prob = sb("prob", [P, 4, 2, QC, S], F32)
        oT = sb("oT", [P, 2, S], F32)
        zinv = sb("zinv", [P, QC, H // 2], F32)
        o_sb = sb("o_sb", [P, NC, D], F32)
        onT = sb("onT", [P, S], F32)
        x1 = sb("x1", [P, NC, D], F32)
        stats2 = sb("stats2", [P, NC, 6], F32)
        mean_var2 = sb("mean_var2", [P, NC, 2], F32)
        vareps2 = sb("vareps2", [P, NC], F32)
        rstd2 = sb("rstd2", [P, NC], F32)
        xn2 = xn
        xh = sb("xh", [P, T], F32R)
        xl = sb("xl", [P, T], F32R)
        gw_sb = sb("gw_sb", [P, E], F32)
        gwh = sb("gwh", [P, E], F32R)
        gwl = sb("gwl", [P, E], F32R)
        gb_sb = sb("gb_sb", [P, E], F32)
        w_sb = sb("w_sb", [P, FF], F32)
        wgh = sb("wgh", [P, FF], F32R)
        wgl = sb("wgl", [P, FF], F32R)
        wuh = sb("wuh", [P, FF], F32R)
        wul = sb("wul", [P, FF], F32R)
        m_flat = m_sb[:, :, :, :, :].rearrange("p a b c k -> p (a b c k)")
        wd_sb = m_flat[:, 0:FF].bitcast(F32).rearrange("p (c d) -> p c d", d=D)
        sel_sb = m_flat[0:PARTS * E, FF:FF + (NI - 1) * P // 2].bitcast(BF16)
        eneg = sb("eneg", [P, NC, E], F32)
        score = sb("score", [P, NC, E], F32)
        choice = sb("choice", [P, NC, E], F32)
        gtop = sb("gtop", [P, NC, NG, 8], F32)
        gscore = sb("gscore", [P, NC, 10], F32)
        gbest = sb("gbest", [P, NC, 8], F32)
        gtake = sb("gtake", [P, NC, 8], F32)
        gleft = sb("gleft", [P, NC, 10], F32)
        gmask = sb("gmask", [P, NC, NG], F32)
        cmask = sb("cmask", [P, NC, E], F32)
        ebest = sb("ebest", [P, NC, 8], F32)
        eleft = sb("eleft", [P, NC, E], F32)
        wsel = sb("wsel", [P, NC, E], F32)
        wsum = sb("wsum", [P, NC], F32)
        winv = sb("winv", [P, NC], F32)
        wfin = sb("wfin", [P, NC, E], F32)
        wrest = sb("wrest", [P, NC, E], F32)
        wparts = sb("wparts", [P, NC, PARTS, E], BF16)
        wT = sb("wT", [PARTS * E, T], BF16)
        prob_flat = prob[:, :, :, :, :].rearrange("p n j c q -> p (n j c q)")
        gate = prob_flat[:, 0:3 * HALF].rearrange("p (n t) -> p n t", n=3)
        gu = prob_flat[:, 3 * HALF:5 * HALF].rearrange("p (n t) -> p n t", n=2)
        hid = prob_flat[:, 5 * HALF:8 * HALF].rearrange("p (n t) -> p n t", n=3)
        yT = xnT

        s_ps = psum("s_ps", [P, 4, 512])
        t_ps = psum("t_ps", [P, 2, 512])
        o_ps = psum("o_ps", [P, 512])
        m_ps = psum("m_ps", [P, 512])
        m_psb = m_ps[:, :].bitcast(BF16)

        d_x, d_wq, d_wk, d_wv, d_wo = (sem(f"loaded_{n}") for n in ("x", "wq", "wk", "wv", "wo"))
        d_ctx, d_id, d_idb, d_bo = (sem(f"loaded_{n}") for n in ("ctx", "ident", "identb", "bo"))
        d_mq = [sem(f"loaded_maskq{b}") for b in range(B)]
        d_mt = [sem(f"loaded_maskT{b}") for b in range(B)]
        d_gw, d_gb, d_wg, d_wu, d_wd, d_sel, d_ones = (sem(f"loaded_{n}") for n in ("gw", "gb", "wg", "wu", "wd", "sel", "ones"))
        q_out = [sem(f"q_parts_in_dram{i}") for i in range(len(SPANS))]
        k_out = [sem(f"k_parts_in_dram{i}") for i in range(len(SPANS))]
        q_in = [sem(f"q_stack_loaded{i}") for i in range(len(SPANS))]
        k_in = [sem(f"k_stack_loaded{i}") for i in range(len(SPANS))]
        m_out = [sem(f"maxima_in_dram{b}") for b in range(B)]
        m_in = [sem(f"maxima_loaded{b}") for b in range(B)]
        pool_set = sem("pool_set")
        bo_added = sem("bo_added")
        bias_ready = sem("bias_ready")
        var_ready = sem("var_ready")
        rstd_ready = sem("rstd_ready")
        xn_ready = sem("xn_ready")
        xnT_ps = sem("xnT_ps")
        xnT_ready = sem("xnT_ready")
        k_ps, q_ps = sem("k_ps"), sem("q_ps")
        k_high, q_high = sem("k_high"), sem("q_high")
        k_rest, q_rest = sem("k_rest"), sem("q_rest")
        k_low, q_low = sem("k_low"), sem("q_low")
        v_ps = sem("v_ps")
        v_ready = sem("v_ready")
        dve_step = sem("dve_step")
        s_ready = sem("s_ready")
        top_ready = sem("top_ready")
        ntop_ready = sem("ntop_ready")
        ntopT_ready = sem("ntopT_ready")
        t_ready = sem("t_ready")
        p_ready = sem("p_ready")
        pv_done = sem("pv_done")
        oT_ready = sem("oT_ready")
        m_written = sem("m_written")
        m_read = sem("m_read")
        o_ready = sem("o_ready")
        onT_ready = sem("onT_ready")
        x1_ready = sem("x1_ready")
        var2_ready = sem("var2_ready")
        rstd2_ready = sem("rstd2_ready")
        xn2_ready = sem("xn2_ready")
        xh_ready, xl_ready = sem("xh_ready"), sem("xl_ready")
        w_split = sem("w_split")
        gw_split = sem("gw_split")
        eneg_ready = sem("eneg_ready")
        wparts_ready = sem("wparts_ready")
        wT_ready = sem("wT_ready")
        g_ready, u_ready, wb_ready = sem("g_ready"), sem("u_ready"), sem("wb_ready")
        gate_ready = sem("gate_ready")
        gu_ready = sem("gu_ready")
        hid_ready = sem("hid_ready")
        down_done = sem("down_done")
        yT_ready = sem("yT_ready")
        stored = sem("stored")

        uses = [("xnT", 0), ("xnT", 1), ("xnT", 2)]

        def tail(b):
            return [("on", b), ("proj", b), ("xn2T", b), ("logit", b)]

        uses += [("ntop", 0)]
        for b in range(B):
            if b >= 1:
                uses += [("o", b - 1, 1), ("on", b - 1)]
            if b + 1 < B:
                uses += [("ntop", b + 1)]
            if b >= 1:
                uses += [("proj", b - 1), ("xn2T", b - 1)]
            uses += [("o", b, 0)]
            if b >= 1:
                uses += [("logit", b - 1)]
            if b == B - 1:
                uses += [("wT", 0)]
        uses += [("o", B - 1, 1)] + tail(B - 1) + [("wT", 1)]

        def use(*key):
            return uses.index(tuple(key))

        pair_col = [(b, p) for b in range(B) for p in range(PAIRS)]
        NP = len(pair_col)

        def span_of(b):
            return min(b, 2)

        block = ctx.enter_context(nc.Block())

        @block.sync
        def _(sp):
            xv = x.rearrange("(c p) d -> p c d", p=P)
            sp.dma_start(mq_sb[:, 0, :, :], maskq[0].rearrange("(c p) k -> p c k", p=P)).then_inc(d_mq[0], 16)
            sp.dma_start(x_sb[:, :, :], xv).then_inc(d_x, 16)
            sp.dma_start(wk_sb[:, :], wkT).then_inc(d_wk, 16)
            sp.dma_start(ctxT_sb[:, :], ctxT).then_inc(d_ctx, 16)
            sp.dma_start(id_sb[:, :], ident).then_inc(d_id, 16)
            sp.dma_start(wq_sb[:, :], wqT).then_inc(d_wq, 16)
            sp.dma_start(wv_sb[:, :], wvT).then_inc(d_wv, 16)
            sp.dma_start(idb_sb[:, :], identb).then_inc(d_idb, 16)
            for b in range(1, B):
                sp.dma_start(mq_sb[:, b, :, :], maskq[b].rearrange("(c p) k -> p c k", p=P)).then_inc(d_mq[b], 16)

            def parts_out(i, parts, dram, low, out):
                t0, n = SPANS[i]
                sp.wait_ge(low, i + 1)
                for blk, first, count in ((0, 0, 3), (3, 0, 2), (5, 0, 1)):
                    sp.dma_start(dram[blk:blk + count, :, t0:t0 + n].rearrange("c r t -> r c t"),
                                 parts[:, first:first + count, t0:t0 + n]).then_inc(out, 16)

            def k_parts_out(i):
                t0, n = SPANS[i]
                sp.wait_ge(k_low, i + 1)
                for blk, part in enumerate((0, 0, 0, 1, 1, 2)):
                    sp.dma_start(k_dram[blk, :, t0:t0 + n], kp[:, part, t0:t0 + n]).then_inc(k_out[i], 16)

            def stack_in(i, dram, out, out_n, stack, in_):
                t0, n = SPANS[i]
                sp.wait_ge(out, out_n)
                src = dram.rearrange("c (d p j) t -> j (c d) p t", d=DK, j=2)
                for j in range(2):
                    sp.dma_start(stack[HALFP * j:HALFP * j + STACK, :, t0:t0 + n],
                                 src[j, :, :, t0:t0 + n]).then_inc(in_, 16)

            for i in range(len(SPANS)):
                k_parts_out(i)
                parts_out(i, qp, q_dram, q_low, q_out[i])
                stack_in(i, k_dram, k_out[i], 96, ks, k_in[i])
                stack_in(i, q_dram, q_out[i], 48, qs, q_in[i])
                if i == 0:
                    for j in range(2):
                        sp.dma_start(ks[HALFP * j + STACK:HALFP * j + STACKM, :, :],
                                     ones.rearrange("c (p t) -> c p t", p=PAIRS)).then_inc(d_ones, 16)
                    for b in range(B):
                        sp.dma_start(mt_sb[:, b, :, :], maskT[b].rearrange("(c p) k -> p c k", p=P)).then_inc(d_mt[b], 16)
                    sp.dma_start(bo_sb[:, :], bo.partition_broadcast(P)).then_inc(d_bo, 16)
                    sp.dma_start(wo_sb[:, :], woT).then_inc(d_wo, 16)
            sp.dma_start(gw_sb[:, :], gwT).then_inc(d_gw, 16)
            sp.dma_start(gb_sb[:, :], gbias.partition_broadcast(P)).then_inc(d_gb, 16)
            sp.dma_start(w_sb[:, :], wgT).then_inc(d_wg, 16)
            sp.wait_ge(bias_ready, 2 * B)
            sp.dma_start(wd_sb[:, :, :], wdT.rearrange("(c p) d -> p c d", p=P)).then_inc(d_wd, 16)
            sp.dma_start(sel_sb, sel).then_inc(d_sel, 16)
            for b in range(B):
                sp.wait_ge(ntopT_ready, b + 1)
                sp.dma_start(m_dram[b], ntopT[:, b % 2, :]).then_inc(m_out[b], 16)
                sp.wait_ge(m_out[b], 16)
                src = m_dram[b].rearrange("(c p j) t -> j c p t", c=PARTS, j=2)
                for j in range(2):
                    sp.dma_start(qs[HALFP * j + STACK:HALFP * j + STACKM, :, b * S:(b + 1) * S],
                                 src[j]).then_inc(m_in[b], 16)
            for f in range(2):
                sp.wait_ge(yT_ready, f + 1)
                sp.dma_start(outT[:, f * HALF:(f + 1) * HALF], yT[:, f * HALF:(f + 1) * HALF]).then_inc(stored, 16)
            sp.wait_ge(stored, 32)

        @block.gpsimd
        def _(pool):
            nc.gpsimd.memset(minus_half[:, :], -0.5).then_inc(pool_set, 1)
            pool.wait_ge(pool_set, 1)

            for n, (a, e) in enumerate(((0, QC), (QC, NC))):
                pool.wait_ge(var_ready, n + 1)
                nc.gpsimd.tensor_tensor(rstd[:, a:e], vareps[:, a:e], minus_half[:, a:e], ALU.pow).then_inc(rstd_ready, 1)

            nc.gpsimd.memset(vs[:, :, :, DK:DK + 1], 1.0)
            nc.gpsimd.memset(vs[:, :, :, DK + 1:VW], 0.0)
            nc.gpsimd.memset(gscore[:, :, NG:10], FILL)
            nc.gpsimd.memset(gtake[:, :, 2:8], FILL).then_inc(pool_set, 1)
            pool.wait_ge(d_bo, 16)
            pool.wait_ge(xn_ready, NC)
            for c in range(NC):
                last = nc.gpsimd.tensor_tensor(xb_sb[:, c, :], x_sb[:, c, :], bo_sb[:, :], ALU.add)
            last.then_inc(bo_added, 1)
            pool.wait_ge(d_gw, 16)
            nc.gpsimd.tensor_copy(gwh[:, :], gw_sb[:, :]).then_inc(gw_split, 1)
            pool.wait_ge(gw_split, 1)
            nc.gpsimd.tensor_tensor(gwl[:, :], gw_sb[:, :], gwh[:, :].bitcast(F32), ALU.subtract).then_inc(gw_split, 1)
            n = 0

            def rstd2_step(b):
                pool.wait_ge(var2_ready, b + 1)
                cs = slice(QC * b, QC * b + QC)
                nc.gpsimd.tensor_tensor(rstd2[:, cs], vareps2[:, cs], minus_half[:, cs], ALU.pow).then_inc(rstd2_ready, 1)

            for loaded, hi, lo in ((d_wg, wgh, wgl), (d_wu, wuh, wul)):
                pool.wait_ge(loaded, 16)
                nc.gpsimd.tensor_copy(hi[:, :], w_sb[:, :]).then_inc(w_split, 1)
                n += 1
                pool.wait_ge(w_split, n)
                nc.gpsimd.tensor_tensor(lo[:, :], w_sb[:, :], hi[:, :].bitcast(F32), ALU.subtract).then_inc(w_split, 1)
                n += 1
                if loaded is d_wg:
                    pool.wait_ge(w_split, n)
                    pool.dma_start(w_sb[:, :], wuT).then_inc(d_wu, 16)
            for b in range(B):
                rstd2_step(b)

        @block.tensor
        def _(pe):
            def m_use(*key):
                n = use(*key)
                if n:
                    pe.wait_ge(m_read, n)

            def k_proj(i):
                t0, n = SPANS[i]
                if i:
                    pe.wait_ge(k_rest, i)
                nc.tensor.matmul(t_ps[:, 0, 0:n], wk_sb[:, :], ctxT_sb[:, t0:t0 + n],
                                 start=True, stop=True).then_inc(k_ps, 1)

            def x_transposes(i):
                t0, n = SPANS[i]
                m_use("xnT", i)
                pe.wait_ge(xn_ready, (t0 + n) // P)
                for c in range(n // P):
                    last = nc.tensor.transpose(m_ps[:, c * P:(c + 1) * P], xn[:, t0 // P + c, :], id_sb[:, :])
                last.then_inc(m_written, 1)

            def q_proj(i):
                t0, n = SPANS[i]
                pe.wait_ge(xnT_ready, i + 1)
                if i:
                    pe.wait_ge(q_rest, i)
                nc.tensor.matmul(t_ps[:, 1, 0:n], wq_sb[:, :], xnT[:, t0:t0 + n],
                                 start=True, stop=True).then_inc(q_ps, 1)

            def v_proj(i):
                if i:
                    pe.wait_ge(v_ready, i)
                for c in range(4):
                    last = nc.tensor.matmul(o_ps[:, c * P:(c + 1) * P],
                                            ctxT_sb[:, (4 * i + c) * P:(4 * i + c + 1) * P], wv_sb[:, :],
                                            start=True, stop=True)
                last.then_inc(v_ps, 1)

            def scores(n):
                b, p = pair_col[n]
                t0 = b * S
                r = 2 * (n % 2)
                if n >= 2:
                    pe.wait_ge(top_ready, n - 1)
                if p == 0:
                    pe.wait_ge(bias_ready, 2 * b + 1)
                    pe.wait_ge(k_in[span_of(b)], 32)
                    pe.wait_ge(q_in[span_of(b)], 32)
                for j in range(2):
                    nc.tensor.matmul(s_ps[:, r + j, :], idb_sb[:, :], biasq[:, b, :, :],
                                     start=True, stop=False, skip_group_check=True)
                for c in range(QC):
                    for j in range(2):
                        rows = slice(HALFP * j, HALFP * j + STACK)
                        last = nc.tensor.matmul(s_ps[:, r + j, c * S:(c + 1) * S],
                                                qs[rows, p, t0 + c * P:t0 + (c + 1) * P],
                                                ks[rows, p, t0:t0 + S],
                                                start=False, stop=True, skip_group_check=True)
                last.then_inc(s_ready, 1)

            def scores_t(n):
                b, p = pair_col[n]
                t0 = b * S
                if n >= 1:
                    pe.wait_ge(p_ready, n)
                if n == 0:
                    pe.wait_ge(k_rest, len(SPANS))
                    pe.wait_ge(q_rest, len(SPANS))
                    pe.wait_ge(d_ones, 32)
                if p == 0:
                    pe.wait_ge(bias_ready, 2 * b + 2)
                    pe.wait_ge(m_in[b], 32)
                for j in range(2):
                    nc.tensor.matmul(t_ps[:, j, :], idb_sb[:, :], biast[:, b, :, :],
                                     start=True, stop=False, skip_group_check=True)
                for c in range(QC):
                    for j in range(2):
                        rows = slice(HALFP * j, HALFP * j + STACKM)
                        last = nc.tensor.matmul(t_ps[:, j, c * S:(c + 1) * S],
                                                ks[rows, p, t0 + c * P:t0 + (c + 1) * P],
                                                qs[rows, p, t0:t0 + S],
                                                start=False, stop=True, skip_group_check=True)
                last.then_inc(t_ready, 1)

            def pv(q):
                b, g = divmod(q, 4)
                pe.wait_ge(p_ready, 2 * q + 2)
                if q == 0:
                    pe.wait_ge(v_ready, 2)
                    pe.wait_ge(pool_set, 2)
                if q >= 2 and q % 2 == 0:
                    pe.wait_ge(oT_ready, q // 2)
                for c in range(QC):
                    for j in range(4):
                        n = 2 * q + j // 2
                        last = nc.tensor.matmul(o_ps[32 * j:32 * j + VW, (g % 2) * S:(g % 2 + 1) * S],
                                                vs[:, QC * b + c, 4 * g + j, :],
                                                prob[:, n % 4, j % 2, c, :],
                                                start=(c == 0), stop=(c == QC - 1))
                last.then_inc(pv_done, 1)

            def ntop_transpose(b):
                m_use("ntop", b)
                pe.wait_ge(ntop_ready, b + 1)
                for c in range(QC):
                    last = nc.tensor.transpose(m_psb[0:PARTS * H, c * P:(c + 1) * P], ntop[:, c, :, :], idb_sb[:, :])
                last.then_inc(m_written, 1)

            def o_transpose(b, half):
                m_use("o", b, half)
                pe.wait_ge(oT_ready, 2 * b + half + 1)
                for c in range(QC):
                    for g in range(2):
                        last = nc.tensor.transpose(m_ps[:, (2 * c + g) * P:(2 * c + g + 1) * P],
                                                   oT[:, g, c * P:(c + 1) * P], id_sb[:, :])
                last.then_inc(m_written, 1)

            def on_transpose(b):
                m_use("on", b)
                pe.wait_ge(o_ready, 2 * b + 2)
                for c in range(QC):
                    last = nc.tensor.transpose(m_ps[:, c * P:(c + 1) * P], o_sb[:, QC * b + c, :], id_sb[:, :])
                last.then_inc(m_written, 1)

            def out_proj(b):
                m_use("proj", b)
                pe.wait_ge(onT_ready, b + 1)
                if b == 0:
                    pe.wait_ge(d_wo, 16)
                for c in range(QC):
                    last = nc.tensor.matmul(m_ps[:, c * P:(c + 1) * P], onT[:, c * P:(c + 1) * P], wo_sb[:, :],
                                            start=True, stop=True)
                last.then_inc(m_written, 1)

            def xn2_transpose(b):
                m_use("xn2T", b)
                pe.wait_ge(xn2_ready, b + 1)
                for c in range(QC):
                    last = nc.tensor.transpose(m_ps[:, c * P:(c + 1) * P], xn2[:, QC * b + c, :], id_sb[:, :])
                last.then_inc(m_written, 1)

            def logits(b):
                m_use("logit", b)
                pe.wait_ge(xl_ready, b + 1)
                if b == 0:
                    pe.wait_ge(gw_split, 2)
                for c in range(QC):
                    t = slice((QC * b + c) * P, (QC * b + c + 1) * P)
                    out = m_ps[:, c * E:(c + 1) * E]
                    nc.tensor.matmul(out, xh[:, t], gwh[:, :], start=True, stop=False)
                    nc.tensor.matmul(out, xh[:, t], gwl[:, :], start=False, stop=False)
                    last = nc.tensor.matmul(out, xl[:, t], gwh[:, :], start=False, stop=True)
                last.then_inc(m_written, 1)

            def w_transpose(f):
                m_use("wT", f)
                pe.wait_ge(wparts_ready, f + 1)
                for c in range(HC):
                    last = nc.tensor.transpose(m_psb[0:PARTS * E, c * P:(c + 1) * P],
                                               wparts[:, HC * f + c, :, :], idb_sb[:, :])
                last.then_inc(m_written, 1)

            def y_bank(f):
                return o_ps if f == 0 else m_ps

            def residual(f):
                if f == 0:
                    pe.wait_ge(oT_ready, 2 * B)
                else:
                    m_use("wT", 1)
                    pe.wait_ge(m_read, use("wT", 1) + 1)
                pe.wait_ge(x1_ready, 2 * f + 2)
                for c in range(HC):
                    nc.tensor.matmul(y_bank(f)[:, c * P:(c + 1) * P], x1[:, HC * f + c, :], id_sb[:, :],
                                     start=(c == 0), stop=False, skip_group_check=True)

            def gate_up(f, i):
                k = f * NI + i
                t = slice(f * HALF, (f + 1) * HALF)
                w = slice(i * P, (i + 1) * P)
                if i == 0:
                    pe.wait_ge(xl_ready, 2 * f + 2)
                if k == 0:
                    pe.wait_ge(top_ready, NP)
                    pe.wait_ge(p_ready, NP)
                    pe.wait_ge(w_split, 4)
                    pe.wait_ge(d_sel, 16)
                for r, (hi, lo, ready, free) in enumerate(((wgh, wgl, g_ready, gate_ready),
                                                           (wuh, wul, u_ready, gu_ready))):
                    if k >= 2:
                        pe.wait_ge(free, k - 1)
                    out = s_ps[:, 2 * r + k % 2, :]
                    nc.tensor.matmul(out, hi[:, w], xh[:, t], start=True, stop=False)
                    nc.tensor.matmul(out, hi[:, w], xl[:, t], start=False, stop=False)
                    nc.tensor.matmul(out, lo[:, w], xh[:, t], start=False, stop=True).then_inc(ready, 1)
                if i < NI - 1:
                    if i == 0:
                        pe.wait_ge(wT_ready, f + 1)
                    if k >= 2:
                        pe.wait_ge(hid_ready, k - 1)
                    nc.tensor.matmul(t_ps[:, k % 2, :], sel_sb[:, w], wT[:, t],
                                     start=True, stop=True).then_inc(wb_ready, 1)

            def down(f, i):
                k = f * NI + i
                pe.wait_ge(hid_ready, k + 1)
                if k == 0:
                    pe.wait_ge(d_wd, 16)
                nc.tensor.matmul(y_bank(f)[:, :], wd_sb[:, i, :], hid[:, k % 3, :],
                                 start=False, stop=(i == NI - 1), skip_group_check=True).then_inc(down_done, 1)

            pe.wait_ge(d_wk, 16)
            pe.wait_ge(d_ctx, 16)
            k_proj(0)
            pe.wait_ge(d_id, 16)
            x_transposes(0)
            pe.wait_ge(d_wq, 16)
            q_proj(0)
            pe.wait_ge(d_wv, 16)
            v_proj(0)
            for i in range(1, len(SPANS)):
                k_proj(i)
                x_transposes(i)
                q_proj(i)
            v_proj(1)
            pe.wait_ge(d_idb, 16)
            for n in range(PAIRS):
                scores(n)
            for n in range(PAIRS, AHEAD):
                scores(n)
                if n == PAIRS + 1:
                    ntop_transpose(0)
            for n in range(NP):
                b, p = pair_col[n]
                if n + AHEAD < NP:
                    scores(n + AHEAD)
                scores_t(n)
                if n >= 2 and n % 2 == 0:
                    pv(n // 2 - 1)
                if b >= 1 and p == 1:
                    o_transpose(b - 1, 1)
                if b >= 1 and p == 2:
                    on_transpose(b - 1)
                if b >= 1 and p == 4:
                    out_proj(b - 1)
                if p == 3 and b + 1 < B:
                    ntop_transpose(b + 1)
                if b >= 1 and p == 5:
                    xn2_transpose(b - 1)
                if p == 6:
                    o_transpose(b, 0)
                if b >= 1 and p == 7:
                    logits(b - 1)
            pv(NP // 2 - 1)
            w_transpose(0)
            residual(0)
            steps = {1: lambda: o_transpose(B - 1, 1), 3: lambda: on_transpose(B - 1), 4: lambda: out_proj(B - 1),
                     6: lambda: xn2_transpose(B - 1), 8: lambda: logits(B - 1), 13: lambda: w_transpose(1)}
            for f in range(2):
                if f == 1:
                    residual(1)
                for i in range(NI + 1):
                    if i < NI:
                        gate_up(f, i)
                    if i >= 1:
                        down(f, i - 1)
                    if f == 0 and i in steps:
                        steps[i]()

        @block.scalar
        def _(act):
            def high_mid(i, ps, bank, parts, high, rest_ready, rest, scale):
                t0, n = SPANS[i]
                act.wait_ge(ps, i + 1)
                nc.scalar.activation(parts[:, 0, t0:t0 + n], t_ps[:, bank, 0:n], ACT.Copy, scale=scale).then_inc(high, 1)
                act.wait_ge(rest_ready, i + 1)
                nc.scalar.activation(parts[:, 1, t0:t0 + n], rest[:, 0:n], ACT.Copy).then_inc(high, 1)

            def v_copy(i):
                act.wait_ge(v_ps, i + 1)
                nc.scalar.activation(vs[:, 4 * i:4 * i + 4, :, 0:DK],
                                     o_ps[:, :].rearrange("p (c h d) -> p c h d", c=4, d=DK),
                                     ACT.Copy).then_inc(v_ready, 1)

            def xnT_copy(i):
                t0, n = SPANS[i]
                act.wait_ge(m_written, use("xnT", i) + 1)
                nc.scalar.activation(xnT[:, t0:t0 + n], m_ps[:, 0:n], ACT.Copy).then_inc(m_read, 1)
                act.wait_ge(m_read, use("xnT", i) + 1)
                act.sem_inc(xnT_ready, 1)

            def ntopT_copy(b):
                act.wait_ge(m_written, use("ntop", b) + 1)
                if b >= 2:
                    act.wait_ge(m_out[b - 2], 16)
                nc.scalar.activation(ntopT[:, b % 2, :], m_psb[0:PARTS * H, 0:S], ACT.Copy).then_inc(m_read, 1)
                act.wait_ge(m_read, use("ntop", b) + 1)
                act.sem_inc(ntopT_ready, 1)

            def exp(n):
                act.wait_ge(t_ready, n + 1)
                if n >= 4:
                    act.wait_ge(pv_done, (n - 4) // 2 + 1)
                nc.scalar.activation(prob[:, n % 4, :, :, :].rearrange("p j c q -> p (j c q)"),
                                     t_ps[:, :, :].rearrange("p j q -> p (j q)"), ACT.Exp).then_inc(p_ready, 1)

            def oT_copy(h):
                act.wait_ge(pv_done, 2 * h + 2)
                if h >= 1:
                    act.wait_ge(m_written, use("o", (h - 1) // 2, (h - 1) % 2) + 1)
                nc.scalar.activation(oT[:, :, :].rearrange("p g q -> p (g q)"), o_ps[:, :], ACT.Copy).then_inc(oT_ready, 1)

            def onT_copy(b):
                act.wait_ge(m_written, use("on", b) + 1)
                nc.scalar.activation(onT[:, :], m_ps[:, 0:S], ACT.Copy).then_inc(m_read, 1)
                act.wait_ge(m_read, use("on", b) + 1)
                act.sem_inc(onT_ready, 1)

            def xh_copy(b):
                act.wait_ge(m_written, use("xn2T", b) + 1)
                nc.scalar.activation(xh[:, b * S:(b + 1) * S], m_ps[:, 0:S], ACT.Copy).then_inc(xh_ready, 1)

            def eneg_step(b):
                act.wait_ge(m_written, use("logit", b) + 1)
                nc.scalar.activation(eneg[:, QC * b:QC * b + QC, :].rearrange("p c e -> p (c e)"),
                                     m_ps[:, 0:QC * E], ACT.Exp, scale=-1.0).then_inc(m_read, 1)
                act.wait_ge(m_read, use("logit", b) + 1)
                act.sem_inc(eneg_ready, 1)

            def wT_copy(f):
                act.wait_ge(m_written, use("wT", f) + 1)
                nc.scalar.activation(wT[:, f * HALF:(f + 1) * HALF], m_psb[0:PARTS * E, 0:HALF], ACT.Copy).then_inc(m_read, 1)
                act.wait_ge(m_read, use("wT", f) + 1)
                act.sem_inc(wT_ready, 1)

            def silu(f, i):
                k = f * NI + i
                act.wait_ge(g_ready, k + 1)
                if k >= 3:
                    act.wait_ge(gu_ready, k - 2)
                nc.scalar.activation(gate[:, k % 3, :], s_ps[:, k % 2, :], ACT.Silu).then_inc(gate_ready, 1)

            def y_copy(f):
                act.wait_ge(down_done, (f + 1) * NI)
                bank = o_ps if f == 0 else m_ps
                nc.scalar.activation(yT[:, f * HALF:(f + 1) * HALF], bank[:, :], ACT.Copy).then_inc(yT_ready, 1)

            for i in range(len(SPANS)):
                high_mid(i, k_ps, 0, kp, k_high, k_rest, rest_k, 1.0)
                xnT_copy(i)
                high_mid(i, q_ps, 1, qp, q_high, q_rest, rest_q, QSCALE)
                if i == 0:
                    v_copy(0)
            v_copy(1)
            ntopT_copy(0)
            for n in range(NP):
                b, p = pair_col[n]
                exp(n)
                if n >= 4 and n % 4 == 0:
                    oT_copy(n // 4 - 1)
                if b >= 1 and p == 2:
                    onT_copy(b - 1)
                if p == 3 and b + 1 < B:
                    ntopT_copy(b + 1)
                if b >= 1 and p == 5:
                    xh_copy(b - 1)
                if b >= 1 and p == 7:
                    eneg_step(b - 1)
            oT_copy(NP // 4 - 1)
            wT_copy(0)
            steps = {3: lambda: onT_copy(B - 1), 6: lambda: xh_copy(B - 1), 8: lambda: eneg_step(B - 1),
                     13: lambda: wT_copy(1)}
            for f in range(2):
                for i in range(NI):
                    silu(f, i)
                    if f == 0 and i in steps:
                        steps[i]()
                y_copy(f)

        @block.vector
        def _(dve):
            chain = [0]

            def link(ins):
                chain[0] += 1
                ins.then_inc(dve_step, 1)
                dve.wait_ge(dve_step, chain[0])

            def bias_q(b):
                dve.wait_ge(d_mq[b], 16)
                nc.vector.tensor_scalar(biasq[:, b, :, :], mq_sb[:, b, :, :], 0.0, MASKED,
                                        ALU.is_equal, ALU.mult).then_inc(bias_ready, 1)
                dve.wait_ge(bias_ready, 2 * b + 1)

            def bias_t(b):
                dve.wait_ge(d_mt[b], 16)
                nc.vector.tensor_scalar(biast[:, b, :, :], mt_sb[:, b, :, :], 0.0, MASKED,
                                        ALU.is_equal, ALU.mult).then_inc(bias_ready, 1)

            def keys_left(b):
                cs = slice(QC * b, QC * b + QC)
                link(nc.vector.tensor_reduce(top_bias[:, cs], biasq[:, b, :, :], AX.X, ALU.max))
                link(nc.vector.tensor_scalar(any_key[:, cs], top_bias[:, cs], MASKED, None, ALU.is_gt))

            def moments(a, e, src, st, mv, ve, ready):
                for c in range(a, e):
                    last = nc.vector.bn_stats(st[:, c, :], src[:, c, :])
                link(last)
                for c in range(a, e):
                    last = nc.vector.bn_aggr(mv[:, c, :], st[:, c, :])
                link(last)
                nc.vector.tensor_scalar(ve[:, a:e], mv[:, a:e, 1], EPS, None, ALU.add).then_inc(ready, 1)

            def normalise(i):
                a, e = SPANS[i][0] // P, sum(SPANS[i]) // P
                dve.wait_ge(rstd_ready, min(i, 1) + 1)
                link(nc.vector.tensor_tensor(rs[:, a:e], rstd[:, a:e], any_key[:, a:e], ALU.mult))
                for c in range(a, e):
                    nc.vector.tensor_scalar(xn[:, c, :], x_sb[:, c, :], mean_var[:, c, 0:1], rs[:, c:c + 1],
                                            ALU.subtract, ALU.mult).then_inc(xn_ready, 1)

            def rest_step(i, bank, parts, high, rest_ready, rest, scale):
                t0, n = SPANS[i]
                dve.wait_ge(high, 2 * i + 1)
                nc.vector.scalar_tensor_tensor(out=rest[:, 0:n], in0=t_ps[:, bank, 0:n], scalar=scale,
                                               in1=parts[:, 0, t0:t0 + n], op0=ALU.mult,
                                               op1=ALU.subtract).then_inc(rest_ready, 1)

            def low_step(i, parts, high, rest_ready, rest, low):
                t0, n = SPANS[i]
                dve.wait_ge(high, 2 * i + 2)
                dve.wait_ge(rest_ready, i + 1)
                nc.vector.tensor_tensor(parts[:, 2, t0:t0 + n], rest[:, 0:n], parts[:, 1, t0:t0 + n],
                                        ALU.subtract).then_inc(low, 1)

            def row_max(n):
                b, p = pair_col[n]
                r = 2 * (n % 2)
                dve.wait_ge(s_ready, n + 1)
                nc.vector.tensor_reduce(top[:, b, :, 2 * p:2 * p + 2].rearrange("q c j -> q j c"),
                                        s_ps[:, r:r + 2, :].rearrange("q j (c k) -> q j c k", c=QC),
                                        AX.X, ALU.max).then_inc(top_ready, 1)

            def minus_top(b):
                dve.wait_ge(top_ready, PAIRS * (b + 1))
                if b >= 1:
                    dve.wait_ge(m_written, use("ntop", b - 1) + 1)
                link(nc.vector.tensor_scalar(ntop[:, :, 0, :], top[:, b, :, :], -1.0, None, ALU.mult))
                link(nc.vector.scalar_tensor_tensor(out=top_rest[:, :, :], in0=top[:, b, :, :], scalar=-1.0,
                                                    in1=ntop[:, :, 0, :], op0=ALU.mult, op1=ALU.subtract))
                link(nc.vector.tensor_copy(ntop[:, :, 1, :], top_rest[:, :, :]))
                nc.vector.tensor_tensor(ntop[:, :, 2, :], top_rest[:, :, :], ntop[:, :, 1, :],
                                        ALU.subtract).then_inc(ntop_ready, 1)

            def divide(b, half):
                n = use("o", b, half)
                dve.wait_ge(m_written, n + 1)
                src = m_ps[:, :].rearrange("q (c h w) -> q c h w", c=QC, w=VW)
                link(nc.vector.reciprocal(zinv[:, :, :], src[:, :, :, DK]))
                dst = o_sb[:, QC * b:QC * b + QC, half * D // 2:(half + 1) * D // 2]
                link(nc.vector.tensor_tensor(dst.rearrange("q c (h d) -> q c h d", d=DK), src[:, :, :, 0:DK],
                                             zinv[:, :, :].unsqueeze(3).broadcast_to([P, QC, H // 2, DK]), ALU.mult))
                dve.sem_inc(m_read, 1)
                dve.sem_inc(o_ready, 1)

            def x1_step(b):
                dve.wait_ge(m_written, use("proj", b) + 1)
                if b == 0:
                    dve.wait_ge(bo_added, 1)
                cs = slice(QC * b, QC * b + QC)
                link(nc.vector.tensor_tensor(x1[:, cs, :], m_ps[:, 0:S].rearrange("p (c d) -> p c d", c=QC),
                                             xb_sb[:, cs, :], ALU.add))
                dve.sem_inc(m_read, 1)
                dve.sem_inc(x1_ready, 1)
                moments(QC * b, QC * b + QC, x1, stats2, mean_var2, vareps2, var2_ready)

            def normalise2(b):
                dve.wait_ge(rstd2_ready, b + 1)
                for c in range(QC * b, QC * b + QC):
                    last = nc.vector.tensor_scalar(xn2[:, c, :], x1[:, c, :], mean_var2[:, c, 0:1],
                                                   rstd2[:, c:c + 1], ALU.subtract, ALU.mult)
                last.then_inc(xn2_ready, 1)

            def xl_step(b):
                dve.wait_ge(xh_ready, b + 1)
                t = slice(b * S, (b + 1) * S)
                link(nc.vector.tensor_tensor(xl[:, t], m_ps[:, 0:S], xh[:, t].bitcast(F32), ALU.subtract))
                dve.sem_inc(m_read, 1)
                dve.sem_inc(xl_ready, 1)

            def routing(f):
                cs = slice(HC * f, HC * f + HC)
                chunks = range(HC * f, HC * f + HC)
                dve.wait_ge(eneg_ready, 2 * f + 2)
                if f == 0:
                    dve.wait_ge(d_gb, 16)
                    dve.wait_ge(pool_set, 2)
                link(nc.vector.tensor_scalar(wfin[:, cs, :], eneg[:, cs, :], 1.0, None, ALU.add))
                link(nc.vector.reciprocal(score[:, cs, :], wfin[:, cs, :]))
                link(nc.vector.tensor_tensor(choice[:, cs, :], score[:, cs, :],
                                             gb_sb[:, :].unsqueeze(1).broadcast_to([P, HC, E]), ALU.add))
                for c in chunks:
                    for g in range(NG):
                        last = nc.vector.max(gtop[:, c, g, :], choice[:, c, g * GE:(g + 1) * GE])
                link(last)
                link(nc.vector.tensor_tensor(gscore[:, cs, 0:NG], gtop[:, cs, :, 0], gtop[:, cs, :, 1], ALU.add))
                for c in chunks:
                    last = nc.vector.max(gbest[:, c, :], gscore[:, c, :])
                link(last)
                link(nc.vector.tensor_copy(gtake[:, cs, 0:2], gbest[:, cs, 0:2]))
                for c in chunks:
                    last = nc.vector.match_replace(gleft[:, c, :], gtake[:, c, :], gscore[:, c, :], TAKEN)
                link(last)
                link(nc.vector.tensor_scalar(gmask[:, cs, :], gleft[:, cs, 0:NG], TAKEN, None, ALU.is_equal))
                link(nc.vector.tensor_tensor(cmask[:, cs, :].rearrange("p c (g e) -> p c g e", e=GE),
                                             choice[:, cs, :].rearrange("p c (g e) -> p c g e", e=GE),
                                             gmask[:, cs, :].unsqueeze(3).broadcast_to([P, HC, NG, GE]), ALU.mult))
                for c in chunks:
                    last = nc.vector.max(ebest[:, c, :], cmask[:, c, :])
                link(last)
                for c in chunks:
                    last = nc.vector.match_replace(eleft[:, c, :], ebest[:, c, :], cmask[:, c, :], TAKEN)
                link(last)
                link(nc.vector.scalar_tensor_tensor(out=wsel[:, cs, :], in0=eleft[:, cs, :], scalar=TAKEN,
                                                    in1=score[:, cs, :], op0=ALU.is_equal, op1=ALU.mult))
                link(nc.vector.tensor_reduce(wsum[:, cs], wsel[:, cs, :], AX.X, ALU.add))
                link(nc.vector.tensor_scalar(wsum[:, cs], wsum[:, cs], 1e-20, None, ALU.add))
                link(nc.vector.reciprocal(winv[:, cs], wsum[:, cs]))
                link(nc.vector.scalar_tensor_tensor(out=wfin[:, cs, :], in0=wsel[:, cs, :], scalar=ROUTED_SCALING,
                                                    in1=winv[:, cs].unsqueeze(2).broadcast_to([P, HC, E]),
                                                    op0=ALU.mult, op1=ALU.mult))
                link(nc.vector.tensor_copy(wparts[:, cs, 0, :], wfin[:, cs, :]))
                link(nc.vector.tensor_tensor(wrest[:, cs, :], wfin[:, cs, :], wparts[:, cs, 0, :], ALU.subtract))
                link(nc.vector.tensor_copy(wparts[:, cs, 1, :], wrest[:, cs, :]))
                nc.vector.tensor_tensor(wparts[:, cs, 2, :], wrest[:, cs, :], wparts[:, cs, 1, :],
                                        ALU.subtract).then_inc(wparts_ready, 1)

            def hidden(f, i):
                k = f * NI + i
                dve.wait_ge(gate_ready, k + 1)
                dve.wait_ge(u_ready, k + 1)
                if k >= 3:
                    dve.wait_ge(down_done, k - 2)
                routed = i < NI - 1
                dst = gu[:, k % 2, :] if routed else hid[:, k % 3, :]
                nc.vector.tensor_tensor(dst, s_ps[:, 2 + k % 2, :], gate[:, k % 3, :], ALU.mult).then_inc(gu_ready, 1)
                dve.wait_ge(gu_ready, k + 1)
                if not routed:
                    dve.sem_inc(hid_ready, 1)
                    return
                dve.wait_ge(wb_ready, f * (NI - 1) + i + 1)
                nc.vector.tensor_tensor(hid[:, k % 3, :], t_ps[:, k % 2, :], gu[:, k % 2, :], ALU.mult).then_inc(hid_ready, 1)

            bias_q(0)
            keys_left(0)
            dve.wait_ge(d_x, 16)
            moments(0, QC, x_sb, stats, mean_var, vareps, var_ready)
            rest_step(0, 0, kp, k_high, k_rest, rest_k, 1.0)
            low_step(0, kp, k_high, k_rest, rest_k, k_low)
            normalise(0)
            moments(QC, NC, x_sb, stats, mean_var, vareps, var_ready)
            rest_step(0, 1, qp, q_high, q_rest, rest_q, QSCALE)
            low_step(0, qp, q_high, q_rest, rest_q, q_low)
            for b in range(1, B):
                bias_t(b - 1)
                bias_q(b)
                keys_left(b)
            bias_t(B - 1)
            for i in range(1, len(SPANS)):
                rest_step(i, 0, kp, k_high, k_rest, rest_k, 1.0)
                low_step(i, kp, k_high, k_rest, rest_k, k_low)
                normalise(i)
                rest_step(i, 1, qp, q_high, q_rest, rest_q, QSCALE)
                low_step(i, qp, q_high, q_rest, rest_q, q_low)
            for n in range(PAIRS):
                row_max(n)
            minus_top(0)
            for n in range(PAIRS, AHEAD):
                row_max(n)
            for n in range(NP):
                b, p = pair_col[n]
                if n + AHEAD < NP:
                    row_max(n + AHEAD)
                    if (n + AHEAD) % PAIRS == PAIRS - 1:
                        minus_top((n + AHEAD) // PAIRS)
                if b >= 1 and p == 1:
                    divide(b - 1, 1)
                if b >= 1 and p == 4:
                    x1_step(b - 1)
                    normalise2(b - 1)
                if b >= 1 and p == 5:
                    xl_step(b - 1)
                if p == 6:
                    divide(b, 0)
                if b == 2 and p == 7:
                    pass
            routing(0)
            steps = {2: lambda: divide(B - 1, 1), 5: lambda: (x1_step(B - 1), normalise2(B - 1)),
                     7: lambda: xl_step(B - 1), 9: lambda: routing(1)}
            for f in range(2):
                for i in range(NI):
                    if f == 0 and i in steps:
                        steps[i]()
                    hidden(f, i)


_OUT = "outT"


def kernel(**inputs):
    import ml_dtypes
    import concourse.bacc as bacc
    from concourse.bass_utils import run_bass_kernel_spmd

    a = {k: np.asarray(v) for k, v in inputs.items()}
    bf = ml_dtypes.bfloat16

    def by_feature(w):
        return w.reshape(H, DK, D).transpose(2, 1, 0).reshape(D, D)

    select = np.zeros((PARTS, E, NI - 1, 2, I), bf)
    for i in range(NI - 1):
        for j in range(2):
            select[:, 2 * i + j, i, j, :] = 1
    arrays = {
        "x": a["x"].reshape(T, D),
        "ctxT": a["ctx_1024"].reshape(T, D).T,
        "wqT": by_feature(a["L0_xattn_w_q"]),
        "wkT": by_feature(a["L0_xattn_w_k"]),
        "wvT": a["L0_xattn_w_v"].T,
        "woT": a["L0_xattn_w_o"].T,
        "bo": a["L0_xattn_b_o"],
        "maskq": a["mask_BxSxS2_ik0"],
        "maskT": a["mask_BxSxS2_ik0"].transpose(0, 2, 1),
        "gwT": a["L0_ffn_gate_w"].T,
        "gbias": a["L0_ffn_gate_bias"],
        "wgT": np.concatenate([a["L0_ffn_expert_gate"].reshape(E * I, D), a["L0_ffn_shared_gate"]]).T,
        "wuT": np.concatenate([a["L0_ffn_expert_up"].reshape(E * I, D), a["L0_ffn_shared_up"]]).T,
        "wdT": np.concatenate([a["L0_ffn_expert_down"].transpose(0, 2, 1).reshape(E * I, D),
                               a["L0_ffn_shared_down"].T]),
        "ident": np.eye(P, dtype=np.float32),
        "identb": np.eye(P).astype(bf),
        "sel": select.reshape(PARTS * E, (NI - 1) * P),
        "ones": np.ones((PARTS, PAIRS * T), bf),
    }
    arrays = {f"in_{k}": np.ascontiguousarray(v) for k, v in arrays.items()}
    nc = bacc.Bacc("TRN2", target_bir_lowering=False, num_devices=1)
    args = [nc.dram_tensor(k, v.shape, mybir.dt.from_np(v.dtype), kind="ExternalInput").ap()
            for k, v in arrays.items()]
    scratch = [nc.dram_tensor("q_blocks", [BLOCKS, P, T], BF16, kind="Internal").ap(),
               nc.dram_tensor("k_blocks", [BLOCKS, P, T], BF16, kind="Internal").ap(),
               nc.dram_tensor("maxima", [B, PARTS * H, S], BF16, kind="Internal").ap()]
    out = nc.dram_tensor(_OUT, [D, T], F32, kind="ExternalOutput").ap()
    build(nc, *args, *scratch, out)
    r = run_bass_kernel_spmd(nc, [arrays], core_ids=[0])
    return r.results[0][_OUT].T.reshape(B, S, D)
```

```python
from contextlib import ExitStack

import numpy as np

import concourse.bass as bass
from concourse import mybir

F32 = mybir.dt.float32
F32R = mybir.dt.float32r
BF16 = mybir.dt.bfloat16
I32 = mybir.dt.int32
ALU = mybir.AluOpType
ACT = mybir.ActivationFunctionType
AX = mybir.AxisListType

P = 128
B, S, D = 4, 256, 128
H, DK = 16, 8
T = B * S
NC = T // P
QC = S // P
PAIRS = H // 2
PARTS = 3
BLOCKS = 6
STACK = BLOCKS * DK
STACKM = STACK + PARTS
HALFP = P // 2
VW = 32
E, I = 32, 64
NG, GE = 4, 8
TOPK = 8
FF = E * I + 2 * I
NI = FF // P
HALF = T // 2
HC = HALF // P
MASKED = -float(2**30)
QSCALE = float(1.0 / np.sqrt(np.float32(DK)))
EPS = 1e-5
ROUTED_SCALING = 2.5
FILL = -3.0e38
TAKEN = 3.0e38
AHEAD = 12

SPANS = [(0, S), (S, S), (2 * S, 2 * S)]


def build(nc, x, ctxT, wqT, wkT, wvT, woT, bo, maskq, maskT, gwT, gbias, wgT, wuT, wdT,
          ident, identb, sel, ones, qk_dram, m_dram, outT):
    with ExitStack() as ctx:
        def sb(name, shape, dt):
            return ctx.enter_context(nc.sbuf_tensor(name, shape, dt))

        def psum(name, shape, dt=F32):
            return ctx.enter_context(nc.psum_tensor(name, shape, dt))

        def sem(name):
            return ctx.enter_context(nc.semaphore(name))

        x_sb = sb("x_sb", [P, NC, D], F32)
        xb_sb = x_sb
        bo_sb = sb("bo_sb", [P, D], F32)
        ctxT_sb = sb("ctxT_sb", [P, T], F32)
        wq_sb = sb("wq_sb", [P, P], F32)
        wk_sb = sb("wk_sb", [P, P], F32)
        wv_sb = sb("wv_sb", [P, P], F32)
        wo_sb = sb("wo_sb", [P, P], F32)
        id_sb = sb("id_sb", [P, P], F32)
        idb_sb = sb("idb_sb", [P, P], BF16)
        m_sb = sb("m_sb", [P, 2, B, QC, S], I32)
        mq_sb, mt_sb = m_sb[:, 0], m_sb[:, 1]
        biasq = sb("biasq", [P, B, QC, S], BF16)
        biast = sb("biast", [P, B, QC, S], BF16)
        top_bias = sb("top_bias", [P, NC], F32)
        any_key = sb("any_key", [P, NC], F32)
        stats = sb("stats", [P, NC, 6], F32)
        mean_var = sb("mean_var", [P, NC, 2], F32)
        vareps = sb("vareps", [P, NC], F32)
        rstd = sb("rstd", [P, NC], F32)
        rs = sb("rs", [P, NC], F32)
        minus_half = sb("minus_half", [P, NC], F32)
        xn = sb("xn", [P, NC, D], F32)
        xnT = sb("xnT", [P, T], F32)
        qp = sb("qp", [P, PARTS, T], BF16)
        kp = sb("kp", [P, PARTS, T], BF16)
        rest_q = sb("rest_q", [P, HALF], F32)
        rest_k = sb("rest_k", [P, HALF], F32)
        stack = sb("stack", [P, PAIRS, 2, T], BF16)
        vs = sb("vs", [P, NC, H, VW], F32)
        top = sb("top", [P, B, QC, H], F32)
        top_rest = sb("top_rest", [P, QC, H], F32)
        ntop = sb("ntop", [P, QC, PARTS, H], BF16)
        ntopT = sb("ntopT", [PARTS * H, 2, S], BF16)
        prob = sb("prob", [P, 4, 2, QC, S], F32)
        oT = sb("oT", [P, 2, S], F32)
        zinv = sb("zinv", [P, QC, H // 2], F32)
        o_sb = sb("o_sb", [P, NC, D], F32)
        onT = sb("onT", [P, S], F32)
        x1 = sb("x1", [P, NC, D], F32)
        stats2 = sb("stats2", [P, NC, 6], F32)
        mean_var2 = sb("mean_var2", [P, NC, 2], F32)
        vareps2 = sb("vareps2", [P, NC], F32)
        rstd2 = sb("rstd2", [P, NC], F32)
        xn2 = xn
        xh = sb("xh", [P, T], F32R)
        xl = sb("xl", [P, T], F32R)
        gw_sb = sb("gw_sb", [P, E], F32)
        gwh = sb("gwh", [P, E], F32R)
        gwl = sb("gwl", [P, E], F32R)
        gb_sb = sb("gb_sb", [P, E], F32)
        w_sb = sb("w_sb", [P, FF], F32)
        wgh = sb("wgh", [P, FF], F32R)
        wgl = sb("wgl", [P, FF], F32R)
        wuh = sb("wuh", [P, FF], F32R)
        wul = sb("wul", [P, FF], F32R)
        m_flat = m_sb[:, :, :, :, :].rearrange("p a b c k -> p (a b c k)")
        wd_sb = m_flat[:, 0:FF].bitcast(F32).rearrange("p (c d) -> p c d", d=D)
        sel_sb = m_flat[0:PARTS * E, FF:FF + (NI - 1) * P // 2].bitcast(BF16)
        eneg = sb("eneg", [P, NC, E], F32)
        score = sb("score", [P, NC, E], F32)
        choice = sb("choice", [P, NC, E], F32)
        gtop = sb("gtop", [P, NC, NG, 8], F32)
        gscore = sb("gscore", [P, NC, 10], F32)
        gbest = sb("gbest", [P, NC, 8], F32)
        gtake = sb("gtake", [P, NC, 8], F32)
        gleft = sb("gleft", [P, NC, 10], F32)
        gmask = sb("gmask", [P, NC, NG], F32)
        cmask = sb("cmask", [P, NC, E], F32)
        ebest = sb("ebest", [P, NC, 8], F32)
        eleft = sb("eleft", [P, NC, E], F32)
        wsel = sb("wsel", [P, NC, E], F32)
        wsum = sb("wsum", [P, NC], F32)
        winv = sb("winv", [P, NC], F32)
        wfin = sb("wfin", [P, NC, E], F32)
        wrest = sb("wrest", [P, NC, E], F32)
        wparts = sb("wparts", [P, NC, PARTS, E], BF16)
        wT = sb("wT", [PARTS * E, T], BF16)
        prob_flat = prob[:, :, :, :, :].rearrange("p n j c q -> p (n j c q)")
        gate = prob_flat[:, 0:3 * HALF].rearrange("p (n t) -> p n t", n=3)
        gu = prob_flat[:, 3 * HALF:5 * HALF].rearrange("p (n t) -> p n t", n=2)
        hid = prob_flat[:, 5 * HALF:8 * HALF].rearrange("p (n t) -> p n t", n=3)
        yT = xnT

        s_ps = psum("s_ps", [P, 4, 512])
        t_ps = psum("t_ps", [P, 2, 512])
        o_ps = psum("o_ps", [P, 512])
        m_ps = psum("m_ps", [P, 512])
        m_psb = m_ps[:, :].bitcast(BF16)

        d_xrest, d_ctxrest = sem("loaded_x_rest"), sem("loaded_ctx_rest")
        d_x, d_wq, d_wk, d_wv, d_wo = (sem(f"loaded_{n}") for n in ("x", "wq", "wk", "wv", "wo"))
        d_ctx, d_id, d_idb, d_bo = (sem(f"loaded_{n}") for n in ("ctx", "ident", "identb", "bo"))
        d_mq = [sem(f"loaded_maskq{b}") for b in range(B)]
        d_mt = [sem(f"loaded_maskT{b}") for b in range(B)]
        d_gw, d_gb, d_wg, d_wu, d_wd, d_sel, d_ones = (sem(f"loaded_{n}") for n in ("gw", "gb", "wg", "wu", "wd", "sel", "ones"))
        q_out = [sem(f"q_parts_in_dram{i}") for i in range(len(SPANS))]
        k_out = [sem(f"k_parts_in_dram{i}") for i in range(len(SPANS))]
        stack_in = [sem(f"stacks_loaded{i}") for i in range(len(SPANS))]
        m_out = [sem(f"maxima_in_dram{b}") for b in range(B)]
        m_in = [sem(f"maxima_loaded{b}") for b in range(B)]
        pool_set = sem("pool_set")
        bo_added = sem("bo_added")
        biasq_ready = sem("biasq_ready")
        biast_ready = sem("biast_ready")
        var_ready = sem("var_ready")
        rstd_ready = sem("rstd_ready")
        xn_ready = sem("xn_ready")
        xnT_ps = sem("xnT_ps")
        xnT_ready = sem("xnT_ready")
        k_ps, q_ps = sem("k_ps"), sem("q_ps")
        k_high, q_high = sem("k_high"), sem("q_high")
        k_rest, q_rest = sem("k_rest"), sem("q_rest")
        k_low, q_low = sem("k_low"), sem("q_low")
        v_ps = sem("v_ps")
        v_ready = sem("v_ready")
        dve_step = sem("dve_step")
        s_ready = sem("s_ready")
        top_ready = sem("top_ready")
        ntop_ready = sem("ntop_ready")
        ntopT_ready = sem("ntopT_ready")
        t_ready = sem("t_ready")
        p_ready = sem("p_ready")
        pv_done = sem("pv_done")
        oT_ready = sem("oT_ready")
        m_written = sem("m_written")
        m_read = sem("m_read")
        o_ready = sem("o_ready")
        onT_ready = sem("onT_ready")
        x1_ready = sem("x1_ready")
        var2_ready = sem("var2_ready")
        rstd2_ready = sem("rstd2_ready")
        xn2_ready = sem("xn2_ready")
        xh_ready, xl_ready = sem("xh_ready"), sem("xl_ready")
        w_split = sem("w_split")
        gw_split = sem("gw_split")
        eneg_ready = sem("eneg_ready")
        wparts_ready = sem("wparts_ready")
        wT_ready = sem("wT_ready")
        g_ready, u_ready, wb_ready = sem("g_ready"), sem("u_ready"), sem("wb_ready")
        gate_ready = sem("gate_ready")
        gu_ready = sem("gu_ready")
        hid_ready = sem("hid_ready")
        down_done = sem("down_done")
        yT_ready = sem("yT_ready")
        stored = sem("stored")

        uses = [("xnT", 0), ("xnT", 1), ("xnT", 2)]

        uses += [("ntop", 0)]
        for b in range(B):
            if b >= 1:
                uses += [("o", b - 1, 1), ("on", b - 1), ("proj", b - 1)]
            if b + 1 < B:
                uses += [("ntop", b + 1)]
            if b >= 1:
                uses += [("xn2T", b - 1), ("logit", b - 1)]
            uses += [("o", b, 0)]
        uses += [("wT", 0), ("o", B - 1, 1), ("on", B - 1), ("proj", B - 1), ("xn2T", B - 1), ("logit", B - 1), ("wT", 1)]

        def use(*key):
            return uses.index(tuple(key))

        pair_col = [(b, p) for b in range(B) for p in range(PAIRS)]
        NP = len(pair_col)

        def span_of(b):
            return min(b, 2)

        block = ctx.enter_context(nc.Block())

        @block.sync
        def _(sp):
            xv = x.rearrange("(c p) d -> p c d", p=P)
            sp.dma_start(x_sb[:, 0:QC, :], xv[:, 0:QC, :]).then_inc(d_x, 16)
            sp.dma_start(mq_sb[:, 0, :, :], maskq[0].rearrange("(c p) k -> p c k", p=P)).then_inc(d_mq[0], 16)
            sp.dma_start(wk_sb[:, :], wkT).then_inc(d_wk, 16)
            sp.dma_start(ctxT_sb[:, 0:S], ctxT[:, 0:S]).then_inc(d_ctx, 16)
            sp.dma_start(id_sb[:, :], ident).then_inc(d_id, 16)
            sp.dma_start(wq_sb[:, :], wqT).then_inc(d_wq, 16)
            sp.dma_start(x_sb[:, QC:NC, :], xv[:, QC:NC, :]).then_inc(d_xrest, 16)

            def to_dram(which, parts, i, part, count, block, times, out):
                t0, n = SPANS[i]
                src = parts[:, part:part + count, t0:t0 + n]
                if times > 1:
                    src = src.broadcast_to([P, times, n])
                sp.dma_start(qk_dram[block:block + count * times, :, which, t0:t0 + n].rearrange("c r t -> r c t"),
                             src).then_inc(out, 16)

            def k_to_dram(i):
                sp.wait_ge(k_low, i + 1)
                for block, count in ((0, 3), (3, 2), (5, 1)):
                    to_dram(1, kp, i, 0, count, block, 1, k_out[i])

            def q_to_dram(i):
                sp.wait_ge(q_high, 2 * i + 1)
                to_dram(0, qp, i, 0, 1, 0, 3, q_out[i])
                sp.wait_ge(q_high, 2 * i + 2)
                to_dram(0, qp, i, 1, 1, 3, 2, q_out[i])
                sp.wait_ge(q_low, i + 1)
                to_dram(0, qp, i, 2, 1, 5, 1, q_out[i])

            def stacks_back(i):
                t0, n = SPANS[i]
                sp.wait_ge(k_out[i], 48)
                sp.wait_ge(q_out[i], 48)
                src = qk_dram.rearrange("c (d j p) w t -> j (c d) (p w) t", d=DK, j=2)
                for j in range(2):
                    sp.dma_start(stack[HALFP * j:HALFP * j + STACK, :, :, t0:t0 + n].rearrange("r p w t -> r (p w) t"),
                                 src[j, :, :, t0:t0 + n]).then_inc(stack_in[i], 16)

            k_to_dram(0)
            sp.dma_start(ctxT_sb[:, S:T], ctxT[:, S:T]).then_inc(d_ctxrest, 16)
            sp.dma_start(mq_sb[:, 1, :, :], maskq[1].rearrange("(c p) k -> p c k", p=P)).then_inc(d_mq[1], 16)
            q_to_dram(0)
            stacks_back(0)
            sp.dma_start(idb_sb[:, :], identb).then_inc(d_idb, 16)
            sp.dma_start(wv_sb[:, :], wvT).then_inc(d_wv, 16)
            for i in range(1, len(SPANS)):
                k_to_dram(i)
                q_to_dram(i)
                stacks_back(i)
            for b in range(B):
                sp.wait_ge(ntopT_ready, b + 1)
                sp.dma_start(m_dram[b], ntopT[:, b % 2, :]).then_inc(m_out[b], 16)
                sp.wait_ge(m_out[b], 16)
                src = m_dram[b].rearrange("(c p j) t -> j c p t", c=PARTS, j=2)
                for j in range(2):
                    sp.dma_start(stack[HALFP * j + STACK:HALFP * j + STACKM, :, 0, b * S:(b + 1) * S],
                                 src[j]).then_inc(m_in[b], 16)
            for f in range(2):
                sp.wait_ge(yT_ready, f + 1)
                sp.dma_start(outT[:, f * HALF:(f + 1) * HALF], yT[:, f * HALF:(f + 1) * HALF]).then_inc(stored, 16)
            sp.wait_ge(stored, 32)

        @block.gpsimd
        def _(pool):
            nc.gpsimd.memset(minus_half[:, :], -0.5).then_inc(pool_set, 1)
            pool.wait_ge(pool_set, 1)

            for n, (a, e) in enumerate(((0, QC), (QC, NC))):
                pool.wait_ge(var_ready, n + 1)
                nc.gpsimd.tensor_tensor(rstd[:, a:e], vareps[:, a:e], minus_half[:, a:e], ALU.pow).then_inc(rstd_ready, 1)
            for b in range(2, B):
                pool.dma_start(mq_sb[:, b, :, :], maskq[b].rearrange("(c p) k -> p c k", p=P)).then_inc(d_mq[b], 16)
            for b in range(B):
                pool.dma_start(mt_sb[:, b, :, :], maskT[b].rearrange("(c p) k -> p c k", p=P)).then_inc(d_mt[b], 16)
            for j in range(2):
                pool.dma_start(stack[HALFP * j + STACK:HALFP * j + STACKM, :, 1, :],
                               ones.rearrange("c (p t) -> c p t", p=PAIRS)).then_inc(d_ones, 16)
            pool.dma_start(bo_sb[:, :], bo.partition_broadcast(P)).then_inc(d_bo, 16)
            pool.dma_start(wo_sb[:, :], woT).then_inc(d_wo, 16)
            pool.dma_start(gw_sb[:, :], gwT).then_inc(d_gw, 16)
            pool.dma_start(gb_sb[:, :], gbias.partition_broadcast(P)).then_inc(d_gb, 16)

            nc.gpsimd.memset(vs[:, :, :, DK:DK + 1], 1.0)
            nc.gpsimd.memset(vs[:, :, :, DK + 1:VW], 0.0)
            nc.gpsimd.memset(gscore[:, :, NG:10], FILL)
            nc.gpsimd.memset(gtake[:, :, 2:8], FILL).then_inc(pool_set, 1)
            for b in range(B):
                pool.wait_ge(d_mt[b], 16)
                nc.gpsimd.tensor_scalar(biast[:, b, :, :], mt_sb[:, b, :, :], 0.0, MASKED,
                                        ALU.is_equal, ALU.mult).then_inc(biast_ready, 1)
            pool.wait_ge(d_bo, 16)
            pool.wait_ge(xn_ready, NC)
            for c in range(NC):
                last = nc.gpsimd.tensor_tensor(xb_sb[:, c, :], x_sb[:, c, :], bo_sb[:, :], ALU.add)
            last.then_inc(bo_added, 1)
            pool.wait_ge(stack_in[len(SPANS) - 1], 32)
            pool.dma_start(w_sb[:, :], wgT).then_inc(d_wg, 16)
            pool.wait_ge(biasq_ready, B)
            pool.wait_ge(biast_ready, B)
            pool.dma_start(wd_sb[:, :, :], wdT.rearrange("(c p) d -> p c d", p=P)).then_inc(d_wd, 16)
            pool.dma_start(sel_sb, sel).then_inc(d_sel, 16)
            pool.wait_ge(d_gw, 16)
            nc.gpsimd.tensor_copy(gwh[:, :], gw_sb[:, :]).then_inc(gw_split, 1)
            pool.wait_ge(gw_split, 1)
            nc.gpsimd.tensor_tensor(gwl[:, :], gw_sb[:, :], gwh[:, :].bitcast(F32), ALU.subtract).then_inc(gw_split, 1)
            n = 0
            for loaded, hi, lo in ((d_wg, wgh, wgl), (d_wu, wuh, wul)):
                pool.wait_ge(loaded, 16)
                nc.gpsimd.tensor_copy(hi[:, :], w_sb[:, :]).then_inc(w_split, 1)
                n += 1
                pool.wait_ge(w_split, n)
                nc.gpsimd.tensor_tensor(lo[:, :], w_sb[:, :], hi[:, :].bitcast(F32), ALU.subtract).then_inc(w_split, 1)
                n += 1
                if loaded is d_wg:
                    pool.wait_ge(w_split, n)
                    pool.dma_start(w_sb[:, :], wuT).then_inc(d_wu, 16)
            for b in range(B):
                pool.wait_ge(var2_ready, b + 1)
                cs = slice(QC * b, QC * b + QC)
                nc.gpsimd.tensor_tensor(rstd2[:, cs], vareps2[:, cs], minus_half[:, cs], ALU.pow).then_inc(rstd2_ready, 1)

        @block.tensor
        def _(pe):
            def m_use(*key):
                n = use(*key)
                if n:
                    pe.wait_ge(m_read, n)

            def k_proj(i):
                t0, n = SPANS[i]
                if i:
                    pe.wait_ge(d_ctxrest, 16)
                    pe.wait_ge(k_rest, i)
                nc.tensor.matmul(t_ps[:, 0, 0:n], wk_sb[:, :], ctxT_sb[:, t0:t0 + n],
                                 start=True, stop=True).then_inc(k_ps, 1)

            def x_transposes(i):
                t0, n = SPANS[i]
                m_use("xnT", i)
                pe.wait_ge(xn_ready, (t0 + n) // P)
                for c in range(n // P):
                    last = nc.tensor.transpose(m_ps[:, c * P:(c + 1) * P], xn[:, t0 // P + c, :], id_sb[:, :])
                last.then_inc(m_written, 1)

            def q_proj(i):
                t0, n = SPANS[i]
                pe.wait_ge(xnT_ready, i + 1)
                if i:
                    pe.wait_ge(q_rest, i)
                nc.tensor.matmul(t_ps[:, 1, 0:n], wq_sb[:, :], xnT[:, t0:t0 + n],
                                 start=True, stop=True).then_inc(q_ps, 1)

            def v_proj(i):
                if i:
                    pe.wait_ge(v_ready, i)
                for c in range(4):
                    last = nc.tensor.matmul(o_ps[:, c * P:(c + 1) * P],
                                            ctxT_sb[:, (4 * i + c) * P:(4 * i + c + 1) * P], wv_sb[:, :],
                                            start=True, stop=True)
                last.then_inc(v_ps, 1)

            def scores(n):
                b, p = pair_col[n]
                t0 = b * S
                r = 2 * (n % 2)
                if n >= 2:
                    pe.wait_ge(top_ready, n - 1)
                if p == 0:
                    pe.wait_ge(biasq_ready, b + 1)
                    pe.wait_ge(stack_in[span_of(b)], 32)
                for j in range(2):
                    nc.tensor.matmul(s_ps[:, r + j, :], idb_sb[:, :], biasq[:, b, :, :],
                                     start=True, stop=False, skip_group_check=True)
                for c in range(QC):
                    for j in range(2):
                        rows = slice(HALFP * j, HALFP * j + STACK)
                        last = nc.tensor.matmul(s_ps[:, r + j, c * S:(c + 1) * S],
                                                stack[rows, p, 0, t0 + c * P:t0 + (c + 1) * P],
                                                stack[rows, p, 1, t0:t0 + S],
                                                start=False, stop=True, skip_group_check=True)
                last.then_inc(s_ready, 1)

            def scores_t(n):
                b, p = pair_col[n]
                t0 = b * S
                if n >= 1:
                    pe.wait_ge(p_ready, n)
                if n == 0:
                    pe.wait_ge(k_rest, len(SPANS))
                    pe.wait_ge(q_rest, len(SPANS))
                    pe.wait_ge(d_ones, 32)
                if p == 0:
                    pe.wait_ge(biast_ready, b + 1)
                    pe.wait_ge(m_in[b], 32)
                for j in range(2):
                    nc.tensor.matmul(t_ps[:, j, :], idb_sb[:, :], biast[:, b, :, :],
                                     start=True, stop=False, skip_group_check=True)
                for c in range(QC):
                    for j in range(2):
                        rows = slice(HALFP * j, HALFP * j + STACKM)
                        last = nc.tensor.matmul(t_ps[:, j, c * S:(c + 1) * S],
                                                stack[rows, p, 1, t0 + c * P:t0 + (c + 1) * P],
                                                stack[rows, p, 0, t0:t0 + S],
                                                start=False, stop=True, skip_group_check=True)
                last.then_inc(t_ready, 1)

            def pv(q):
                b, g = divmod(q, 4)
                pe.wait_ge(p_ready, 2 * q + 2)
                if q == 0:
                    pe.wait_ge(v_ready, 2)
                    pe.wait_ge(pool_set, 2)
                if q >= 2 and q % 2 == 0:
                    pe.wait_ge(oT_ready, q // 2)
                for c in range(QC):
                    for j in range(4):
                        n = 2 * q + j // 2
                        last = nc.tensor.matmul(o_ps[32 * j:32 * j + VW, (g % 2) * S:(g % 2 + 1) * S],
                                                vs[:, QC * b + c, 4 * g + j, :],
                                                prob[:, n % 4, j % 2, c, :],
                                                start=(c == 0), stop=(c == QC - 1))
                last.then_inc(pv_done, 1)

            def ntop_transpose(b):
                m_use("ntop", b)
                pe.wait_ge(ntop_ready, b + 1)
                for c in range(QC):
                    last = nc.tensor.transpose(m_psb[0:PARTS * H, c * P:(c + 1) * P], ntop[:, c, :, :], idb_sb[:, :])
                last.then_inc(m_written, 1)

            def o_transpose(b, half):
                m_use("o", b, half)
                pe.wait_ge(oT_ready, 2 * b + half + 1)
                for c in range(QC):
                    for g in range(2):
                        last = nc.tensor.transpose(m_ps[:, (2 * c + g) * P:(2 * c + g + 1) * P],
                                                   oT[:, g, c * P:(c + 1) * P], id_sb[:, :])
                last.then_inc(m_written, 1)

            def on_transpose(b):
                m_use("on", b)
                pe.wait_ge(o_ready, 2 * b + 2)
                for c in range(QC):
                    last = nc.tensor.transpose(m_ps[:, c * P:(c + 1) * P], o_sb[:, QC * b + c, :], id_sb[:, :])
                last.then_inc(m_written, 1)

            def out_proj(b):
                m_use("proj", b)
                pe.wait_ge(onT_ready, b + 1)
                if b == 0:
                    pe.wait_ge(d_wo, 16)
                for c in range(QC):
                    last = nc.tensor.matmul(m_ps[:, c * P:(c + 1) * P], onT[:, c * P:(c + 1) * P], wo_sb[:, :],
                                            start=True, stop=True)
                last.then_inc(m_written, 1)

            def xn2_transpose(b):
                m_use("xn2T", b)
                pe.wait_ge(xn2_ready, b + 1)
                for c in range(QC):
                    last = nc.tensor.transpose(m_ps[:, c * P:(c + 1) * P], xn2[:, QC * b + c, :], id_sb[:, :])
                last.then_inc(m_written, 1)

            def logits(b):
                m_use("logit", b)
                pe.wait_ge(xl_ready, b + 1)
                if b == 0:
                    pe.wait_ge(gw_split, 2)
                for c in range(QC):
                    t = slice((QC * b + c) * P, (QC * b + c + 1) * P)
                    out = m_ps[:, c * E:(c + 1) * E]
                    nc.tensor.matmul(out, xh[:, t], gwh[:, :], start=True, stop=False)
                    nc.tensor.matmul(out, xh[:, t], gwl[:, :], start=False, stop=False)
                    last = nc.tensor.matmul(out, xl[:, t], gwh[:, :], start=False, stop=True)
                last.then_inc(m_written, 1)

            def w_transpose(f):
                m_use("wT", f)
                pe.wait_ge(wparts_ready, f + 1)
                for c in range(HC):
                    last = nc.tensor.transpose(m_psb[0:PARTS * E, c * P:(c + 1) * P],
                                               wparts[:, HC * f + c, :, :], idb_sb[:, :])
                last.then_inc(m_written, 1)

            def y_bank(f):
                return o_ps if f == 0 else m_ps

            def residual(f):
                if f == 0:
                    pe.wait_ge(oT_ready, 2 * B)
                else:
                    m_use("wT", 1)
                    pe.wait_ge(m_read, use("wT", 1) + 1)
                pe.wait_ge(x1_ready, 2 * f + 2)
                for c in range(HC):
                    nc.tensor.matmul(y_bank(f)[:, c * P:(c + 1) * P], x1[:, HC * f + c, :], id_sb[:, :],
                                     start=(c == 0), stop=False, skip_group_check=True)

            def gate_up(f, i):
                k = f * NI + i
                t = slice(f * HALF, (f + 1) * HALF)
                w = slice(i * P, (i + 1) * P)
                if i == 0:
                    pe.wait_ge(xl_ready, 2 * f + 2)
                if k == 0:
                    pe.wait_ge(top_ready, NP)
                    pe.wait_ge(p_ready, NP)
                    pe.wait_ge(w_split, 4)
                    pe.wait_ge(d_sel, 16)
                for r, (hi, lo, ready, free) in enumerate(((wgh, wgl, g_ready, gate_ready),
                                                           (wuh, wul, u_ready, gu_ready))):
                    if k >= 2:
                        pe.wait_ge(free, k - 1)
                    out = s_ps[:, 2 * r + k % 2, :]
                    nc.tensor.matmul(out, hi[:, w], xh[:, t], start=True, stop=False)
                    nc.tensor.matmul(out, hi[:, w], xl[:, t], start=False, stop=False)
                    nc.tensor.matmul(out, lo[:, w], xh[:, t], start=False, stop=True).then_inc(ready, 1)
                if i < NI - 1:
                    if i == 0:
                        pe.wait_ge(wT_ready, f + 1)
                    if k >= 2:
                        pe.wait_ge(hid_ready, k - 1)
                    nc.tensor.matmul(t_ps[:, k % 2, :], sel_sb[:, w], wT[:, t],
                                     start=True, stop=True).then_inc(wb_ready, 1)

            def down(f, i):
                k = f * NI + i
                pe.wait_ge(hid_ready, k + 1)
                if k == 0:
                    pe.wait_ge(d_wd, 16)
                nc.tensor.matmul(y_bank(f)[:, :], wd_sb[:, i, :], hid[:, k % 3, :],
                                 start=False, stop=(i == NI - 1), skip_group_check=True).then_inc(down_done, 1)

            pe.wait_ge(d_wk, 16)
            pe.wait_ge(d_ctx, 16)
            k_proj(0)
            pe.wait_ge(d_id, 16)
            x_transposes(0)
            pe.wait_ge(d_wq, 16)
            q_proj(0)
            k_proj(1)
            x_transposes(1)
            q_proj(1)
            pe.wait_ge(d_wv, 16)
            v_proj(0)
            pe.wait_ge(d_idb, 16)
            for n in range(PAIRS):
                scores(n)
                if n == 1:
                    k_proj(2)
                    x_transposes(2)
                if n == 3:
                    q_proj(2)
                    v_proj(1)
            for n in range(PAIRS, AHEAD):
                scores(n)
                if n == PAIRS + 1:
                    ntop_transpose(0)
            for n in range(NP):
                b, p = pair_col[n]
                if n + AHEAD < NP:
                    scores(n + AHEAD)
                scores_t(n)
                if n >= 2 and n % 2 == 0:
                    pv(n // 2 - 1)
                if b >= 1 and p == 1:
                    o_transpose(b - 1, 1)
                if b >= 1 and p == 2:
                    on_transpose(b - 1)
                if b >= 1 and p == 3:
                    out_proj(b - 1)
                if p == 4 and b + 1 < B:
                    ntop_transpose(b + 1)
                if b >= 1 and p == 5:
                    xn2_transpose(b - 1)
                if b >= 1 and p == 6:
                    logits(b - 1)
                if p == 7:
                    o_transpose(b, 0)
            w_transpose(0)
            pv(NP // 2 - 1)
            residual(0)
            steps = {1: lambda: o_transpose(B - 1, 1), 3: lambda: on_transpose(B - 1), 4: lambda: out_proj(B - 1),
                     6: lambda: xn2_transpose(B - 1), 8: lambda: logits(B - 1), 14: lambda: w_transpose(1)}
            for f in range(2):
                if f == 1:
                    residual(1)
                for i in range(NI + 1):
                    if i < NI:
                        gate_up(f, i)
                    if i >= 1:
                        down(f, i - 1)
                    if f == 0 and i in steps:
                        steps[i]()

        @block.scalar
        def _(act):
            def high_mid(i, ps, bank, parts, high, rest_ready, rest, scale):
                t0, n = SPANS[i]
                act.wait_ge(ps, i + 1)
                nc.scalar.activation(parts[:, 0, t0:t0 + n], t_ps[:, bank, 0:n], ACT.Copy, scale=scale).then_inc(high, 1)
                act.wait_ge(rest_ready, i + 1)
                nc.scalar.activation(parts[:, 1, t0:t0 + n], rest[:, 0:n], ACT.Copy).then_inc(high, 1)

            def v_copy(i):
                act.wait_ge(v_ps, i + 1)
                nc.scalar.activation(vs[:, 4 * i:4 * i + 4, :, 0:DK],
                                     o_ps[:, :].rearrange("p (c h d) -> p c h d", c=4, d=DK),
                                     ACT.Copy).then_inc(v_ready, 1)

            def xnT_copy(i):
                t0, n = SPANS[i]
                act.wait_ge(m_written, use("xnT", i) + 1)
                nc.scalar.activation(xnT[:, t0:t0 + n], m_ps[:, 0:n], ACT.Copy).then_inc(m_read, 1)
                act.wait_ge(m_read, use("xnT", i) + 1)
                act.sem_inc(xnT_ready, 1)

            def ntopT_copy(b):
                act.wait_ge(m_written, use("ntop", b) + 1)
                if b >= 2:
                    act.wait_ge(m_out[b - 2], 16)
                nc.scalar.activation(ntopT[:, b % 2, :], m_psb[0:PARTS * H, 0:S], ACT.Copy).then_inc(m_read, 1)
                act.wait_ge(m_read, use("ntop", b) + 1)
                act.sem_inc(ntopT_ready, 1)

            def exp(n):
                act.wait_ge(t_ready, n + 1)
                if n >= 4:
                    act.wait_ge(pv_done, (n - 4) // 2 + 1)
                nc.scalar.activation(prob[:, n % 4, :, :, :].rearrange("p j c q -> p (j c q)"),
                                     t_ps[:, :, :].rearrange("p j q -> p (j q)"), ACT.Exp).then_inc(p_ready, 1)

            def oT_copy(h):
                act.wait_ge(pv_done, 2 * h + 2)
                if h >= 1:
                    act.wait_ge(m_written, use("o", (h - 1) // 2, (h - 1) % 2) + 1)
                nc.scalar.activation(oT[:, :, :].rearrange("p g q -> p (g q)"), o_ps[:, :], ACT.Copy).then_inc(oT_ready, 1)

            def onT_copy(b):
                act.wait_ge(m_written, use("on", b) + 1)
                nc.scalar.activation(onT[:, :], m_ps[:, 0:S], ACT.Copy).then_inc(m_read, 1)
                act.wait_ge(m_read, use("on", b) + 1)
                act.sem_inc(onT_ready, 1)

            def xh_copy(b):
                act.wait_ge(m_written, use("xn2T", b) + 1)
                nc.scalar.activation(xh[:, b * S:(b + 1) * S], m_ps[:, 0:S], ACT.Copy).then_inc(xh_ready, 1)

            def eneg_step(b):
                act.wait_ge(m_written, use("logit", b) + 1)
                nc.scalar.activation(eneg[:, QC * b:QC * b + QC, :].rearrange("p c e -> p (c e)"),
                                     m_ps[:, 0:QC * E], ACT.Exp, scale=-1.0).then_inc(m_read, 1)
                act.wait_ge(m_read, use("logit", b) + 1)
                act.sem_inc(eneg_ready, 1)

            def wT_copy(f):
                act.wait_ge(m_written, use("wT", f) + 1)
                nc.scalar.activation(wT[:, f * HALF:(f + 1) * HALF], m_psb[0:PARTS * E, 0:HALF], ACT.Copy).then_inc(m_read, 1)
                act.wait_ge(m_read, use("wT", f) + 1)
                act.sem_inc(wT_ready, 1)

            def silu(f, i):
                k = f * NI + i
                act.wait_ge(g_ready, k + 1)
                if k >= 3:
                    act.wait_ge(gu_ready, k - 2)
                nc.scalar.activation(gate[:, k % 3, :], s_ps[:, k % 2, :], ACT.Silu).then_inc(gate_ready, 1)

            def y_copy(f):
                act.wait_ge(down_done, (f + 1) * NI)
                bank = o_ps if f == 0 else m_ps
                nc.scalar.activation(yT[:, f * HALF:(f + 1) * HALF], bank[:, :], ACT.Copy).then_inc(yT_ready, 1)

            def spans(i):
                high_mid(i, k_ps, 0, kp, k_high, k_rest, rest_k, 1.0)
                xnT_copy(i)
                high_mid(i, q_ps, 1, qp, q_high, q_rest, rest_q, QSCALE)

            for i in range(len(SPANS)):
                spans(i)
                if i == 1:
                    v_copy(0)
            v_copy(1)
            ntopT_copy(0)
            for n in range(NP):
                b, p = pair_col[n]
                exp(n)
                if n >= 4 and n % 4 == 0:
                    oT_copy(n // 4 - 1)
                if b >= 1 and p == 2:
                    onT_copy(b - 1)
                if p == 4 and b + 1 < B:
                    ntopT_copy(b + 1)
                if b >= 1 and p == 5:
                    xh_copy(b - 1)
                if b >= 1 and p == 6:
                    eneg_step(b - 1)
            wT_copy(0)
            oT_copy(NP // 4 - 1)
            steps = {3: lambda: onT_copy(B - 1), 6: lambda: xh_copy(B - 1), 8: lambda: eneg_step(B - 1),
                     14: lambda: wT_copy(1)}
            for f in range(2):
                for i in range(NI):
                    silu(f, i)
                    if f == 0 and i in steps:
                        steps[i]()
                y_copy(f)

        @block.vector
        def _(dve):
            chain = [0]

            def link(ins):
                chain[0] += 1
                ins.then_inc(dve_step, 1)
                dve.wait_ge(dve_step, chain[0])

            def bias_q(b):
                dve.wait_ge(d_mq[b], 16)
                nc.vector.tensor_scalar(biasq[:, b, :, :], mq_sb[:, b, :, :], 0.0, MASKED,
                                        ALU.is_equal, ALU.mult).then_inc(biasq_ready, 1)
                dve.wait_ge(biasq_ready, b + 1)

            def keys_left(b):
                cs = slice(QC * b, QC * b + QC)
                link(nc.vector.tensor_reduce(top_bias[:, cs], biasq[:, b, :, :], AX.X, ALU.max))
                link(nc.vector.tensor_scalar(any_key[:, cs], top_bias[:, cs], MASKED, None, ALU.is_gt))

            def moments(a, e, src, st, mv, ve, ready):
                for c in range(a, e):
                    last = nc.vector.bn_stats(st[:, c, :], src[:, c, :])
                link(last)
                for c in range(a, e):
                    last = nc.vector.bn_aggr(mv[:, c, :], st[:, c, :])
                link(last)
                nc.vector.tensor_scalar(ve[:, a:e], mv[:, a:e, 1], EPS, None, ALU.add).then_inc(ready, 1)

            def normalise(i):
                a, e = SPANS[i][0] // P, sum(SPANS[i]) // P
                dve.wait_ge(rstd_ready, min(i, 1) + 1)
                link(nc.vector.tensor_tensor(rs[:, a:e], rstd[:, a:e], any_key[:, a:e], ALU.mult))
                for c in range(a, e):
                    nc.vector.tensor_scalar(xn[:, c, :], x_sb[:, c, :], mean_var[:, c, 0:1], rs[:, c:c + 1],
                                            ALU.subtract, ALU.mult).then_inc(xn_ready, 1)

            def rest_step(i, bank, parts, high, rest_ready, rest, scale):
                t0, n = SPANS[i]
                dve.wait_ge(high, 2 * i + 1)
                nc.vector.scalar_tensor_tensor(out=rest[:, 0:n], in0=t_ps[:, bank, 0:n], scalar=scale,
                                               in1=parts[:, 0, t0:t0 + n], op0=ALU.mult,
                                               op1=ALU.subtract).then_inc(rest_ready, 1)

            def low_step(i, parts, high, rest_ready, rest, low):
                t0, n = SPANS[i]
                dve.wait_ge(high, 2 * i + 2)
                dve.wait_ge(rest_ready, i + 1)
                nc.vector.tensor_tensor(parts[:, 2, t0:t0 + n], rest[:, 0:n], parts[:, 1, t0:t0 + n],
                                        ALU.subtract).then_inc(low, 1)

            def row_max(n):
                b, p = pair_col[n]
                r = 2 * (n % 2)
                dve.wait_ge(s_ready, n + 1)
                nc.vector.tensor_reduce(top[:, b, :, 2 * p:2 * p + 2].rearrange("q c j -> q j c"),
                                        s_ps[:, r:r + 2, :].rearrange("q j (c k) -> q j c k", c=QC),
                                        AX.X, ALU.max).then_inc(top_ready, 1)

            def minus_top(b):
                dve.wait_ge(top_ready, PAIRS * (b + 1))
                if b >= 1:
                    dve.wait_ge(m_written, use("ntop", b - 1) + 1)
                link(nc.vector.tensor_scalar(ntop[:, :, 0, :], top[:, b, :, :], -1.0, None, ALU.mult))
                link(nc.vector.scalar_tensor_tensor(out=top_rest[:, :, :], in0=top[:, b, :, :], scalar=-1.0,
                                                    in1=ntop[:, :, 0, :], op0=ALU.mult, op1=ALU.subtract))
                link(nc.vector.tensor_copy(ntop[:, :, 1, :], top_rest[:, :, :]))
                nc.vector.tensor_tensor(ntop[:, :, 2, :], top_rest[:, :, :], ntop[:, :, 1, :],
                                        ALU.subtract).then_inc(ntop_ready, 1)

            def divide(b, half):
                n = use("o", b, half)
                dve.wait_ge(m_written, n + 1)
                src = m_ps[:, :].rearrange("q (c h w) -> q c h w", c=QC, w=VW)
                link(nc.vector.reciprocal(zinv[:, :, :], src[:, :, :, DK]))
                dst = o_sb[:, QC * b:QC * b + QC, half * D // 2:(half + 1) * D // 2]
                link(nc.vector.tensor_tensor(dst.rearrange("q c (h d) -> q c h d", d=DK), src[:, :, :, 0:DK],
                                             zinv[:, :, :].unsqueeze(3).broadcast_to([P, QC, H // 2, DK]), ALU.mult))
                dve.sem_inc(m_read, 1)
                dve.sem_inc(o_ready, 1)

            def x1_step(b):
                dve.wait_ge(m_written, use("proj", b) + 1)
                if b == 0:
                    dve.wait_ge(bo_added, 1)
                cs = slice(QC * b, QC * b + QC)
                link(nc.vector.tensor_tensor(x1[:, cs, :], m_ps[:, 0:S].rearrange("p (c d) -> p c d", c=QC),
                                             xb_sb[:, cs, :], ALU.add))
                dve.sem_inc(m_read, 1)
                dve.sem_inc(x1_ready, 1)
                moments(QC * b, QC * b + QC, x1, stats2, mean_var2, vareps2, var2_ready)

            def normalise2(b):
                dve.wait_ge(rstd2_ready, b + 1)
                for c in range(QC * b, QC * b + QC):
                    last = nc.vector.tensor_scalar(xn2[:, c, :], x1[:, c, :], mean_var2[:, c, 0:1],
                                                   rstd2[:, c:c + 1], ALU.subtract, ALU.mult)
                last.then_inc(xn2_ready, 1)

            def xl_step(b):
                dve.wait_ge(xh_ready, b + 1)
                t = slice(b * S, (b + 1) * S)
                link(nc.vector.tensor_tensor(xl[:, t], m_ps[:, 0:S], xh[:, t].bitcast(F32), ALU.subtract))
                dve.sem_inc(m_read, 1)
                dve.sem_inc(xl_ready, 1)

            def sigmoid_step(f):
                cs = slice(HC * f, HC * f + HC)
                chunks = range(HC * f, HC * f + HC)
                dve.wait_ge(eneg_ready, 2 * f + 2)
                if f == 0:
                    dve.wait_ge(d_gb, 16)
                    dve.wait_ge(pool_set, 2)
                link(nc.vector.tensor_scalar(wfin[:, cs, :], eneg[:, cs, :], 1.0, None, ALU.add))
                link(nc.vector.reciprocal(score[:, cs, :], wfin[:, cs, :]))
                link(nc.vector.tensor_tensor(choice[:, cs, :], score[:, cs, :],
                                             gb_sb[:, :].unsqueeze(1).broadcast_to([P, HC, E]), ALU.add))
                for c in chunks:
                    for g in range(NG):
                        last = nc.vector.max(gtop[:, c, g, :], choice[:, c, g * GE:(g + 1) * GE])
                link(last)

            def groups_step(f):
                cs = slice(HC * f, HC * f + HC)
                chunks = range(HC * f, HC * f + HC)
                link(nc.vector.tensor_tensor(gscore[:, cs, 0:NG], gtop[:, cs, :, 0], gtop[:, cs, :, 1], ALU.add))
                for c in chunks:
                    last = nc.vector.max(gbest[:, c, :], gscore[:, c, :])
                link(last)
                link(nc.vector.tensor_copy(gtake[:, cs, 0:2], gbest[:, cs, 0:2]))
                for c in chunks:
                    last = nc.vector.match_replace(gleft[:, c, :], gtake[:, c, :], gscore[:, c, :], TAKEN)
                link(last)
                link(nc.vector.tensor_scalar(gmask[:, cs, :], gleft[:, cs, 0:NG], TAKEN, None, ALU.is_equal))
                link(nc.vector.tensor_tensor(cmask[:, cs, :].rearrange("p c (g e) -> p c g e", e=GE),
                                             choice[:, cs, :].rearrange("p c (g e) -> p c g e", e=GE),
                                             gmask[:, cs, :].unsqueeze(3).broadcast_to([P, HC, NG, GE]), ALU.mult))

            def experts_step(f):
                cs = slice(HC * f, HC * f + HC)
                chunks = range(HC * f, HC * f + HC)
                for c in chunks:
                    last = nc.vector.max(ebest[:, c, :], cmask[:, c, :])
                link(last)
                for c in chunks:
                    last = nc.vector.match_replace(eleft[:, c, :], ebest[:, c, :], cmask[:, c, :], TAKEN)
                link(last)
                link(nc.vector.scalar_tensor_tensor(out=wsel[:, cs, :], in0=eleft[:, cs, :], scalar=TAKEN,
                                                    in1=score[:, cs, :], op0=ALU.is_equal, op1=ALU.mult))

            def weights_step(f):
                cs = slice(HC * f, HC * f + HC)
                link(nc.vector.tensor_reduce(wsum[:, cs], wsel[:, cs, :], AX.X, ALU.add))
                link(nc.vector.tensor_scalar(wsum[:, cs], wsum[:, cs], 1e-20, None, ALU.add))
                link(nc.vector.reciprocal(winv[:, cs], wsum[:, cs]))
                link(nc.vector.scalar_tensor_tensor(out=wfin[:, cs, :], in0=wsel[:, cs, :], scalar=ROUTED_SCALING,
                                                    in1=winv[:, cs].unsqueeze(2).broadcast_to([P, HC, E]),
                                                    op0=ALU.mult, op1=ALU.mult))
                link(nc.vector.tensor_copy(wparts[:, cs, 0, :], wfin[:, cs, :]))
                link(nc.vector.tensor_tensor(wrest[:, cs, :], wfin[:, cs, :], wparts[:, cs, 0, :], ALU.subtract))
                link(nc.vector.tensor_copy(wparts[:, cs, 1, :], wrest[:, cs, :]))
                nc.vector.tensor_tensor(wparts[:, cs, 2, :], wrest[:, cs, :], wparts[:, cs, 1, :],
                                        ALU.subtract).then_inc(wparts_ready, 1)

            def hidden(f, i):
                k = f * NI + i
                dve.wait_ge(gate_ready, k + 1)
                dve.wait_ge(u_ready, k + 1)
                if k >= 3:
                    dve.wait_ge(down_done, k - 2)
                routed = i < NI - 1
                dst = gu[:, k % 2, :] if routed else hid[:, k % 3, :]
                nc.vector.tensor_tensor(dst, s_ps[:, 2 + k % 2, :], gate[:, k % 3, :], ALU.mult).then_inc(gu_ready, 1)
                dve.wait_ge(gu_ready, k + 1)
                if not routed:
                    dve.sem_inc(hid_ready, 1)
                    return
                dve.wait_ge(wb_ready, f * (NI - 1) + i + 1)
                nc.vector.tensor_tensor(hid[:, k % 3, :], t_ps[:, k % 2, :], gu[:, k % 2, :], ALU.mult).then_inc(hid_ready, 1)

            def span_parts(i):
                rest_step(i, 0, kp, k_high, k_rest, rest_k, 1.0)
                low_step(i, kp, k_high, k_rest, rest_k, k_low)
                normalise(i)
                rest_step(i, 1, qp, q_high, q_rest, rest_q, QSCALE)
                low_step(i, qp, q_high, q_rest, rest_q, q_low)

            dve.wait_ge(d_x, 16)
            moments(0, QC, x_sb, stats, mean_var, vareps, var_ready)
            bias_q(0)
            keys_left(0)
            rest_step(0, 0, kp, k_high, k_rest, rest_k, 1.0)
            normalise(0)
            low_step(0, kp, k_high, k_rest, rest_k, k_low)
            dve.wait_ge(d_xrest, 16)
            moments(QC, NC, x_sb, stats, mean_var, vareps, var_ready)
            rest_step(0, 1, qp, q_high, q_rest, rest_q, QSCALE)
            low_step(0, qp, q_high, q_rest, rest_q, q_low)
            bias_q(1)
            keys_left(1)
            span_parts(1)
            for b in range(2, B):
                bias_q(b)
                keys_left(b)
            row_max(0)
            rest_step(2, 0, kp, k_high, k_rest, rest_k, 1.0)
            normalise(2)
            row_max(1)
            low_step(2, kp, k_high, k_rest, rest_k, k_low)
            row_max(2)
            rest_step(2, 1, qp, q_high, q_rest, rest_q, QSCALE)
            row_max(3)
            low_step(2, qp, q_high, q_rest, rest_q, q_low)
            for n in range(4, PAIRS):
                row_max(n)
            minus_top(0)
            for n in range(PAIRS, AHEAD):
                row_max(n)
            for n in range(NP):
                b, p = pair_col[n]
                if n + AHEAD < NP:
                    row_max(n + AHEAD)
                    if (n + AHEAD) % PAIRS == PAIRS - 1:
                        minus_top((n + AHEAD) // PAIRS)
                if b >= 1 and p == 1:
                    divide(b - 1, 1)
                if b >= 1 and p == 3:
                    x1_step(b - 1)
                if b >= 1 and p == 4:
                    normalise2(b - 1)
                if b >= 1 and p == 5:
                    xl_step(b - 1)
                if p == 7:
                    divide(b, 0)
                if (b, p) == (3, 0):
                    sigmoid_step(0)
                if (b, p) == (3, 1):
                    groups_step(0)
                if (b, p) == (3, 2):
                    experts_step(0)
                if (b, p) == (3, 5):
                    weights_step(0)
            steps = {2: lambda: divide(B - 1, 1), 4: lambda: x1_step(B - 1), 5: lambda: normalise2(B - 1),
                     7: lambda: xl_step(B - 1), 9: lambda: sigmoid_step(1), 10: lambda: groups_step(1),
                     11: lambda: experts_step(1), 12: lambda: weights_step(1)}
            for f in range(2):
                for i in range(NI):
                    if f == 0 and i in steps:
                        steps[i]()
                    hidden(f, i)


_OUT = "outT"


def kernel(**inputs):
    import ml_dtypes
    import concourse.bacc as bacc
    from concourse.bass_utils import run_bass_kernel_spmd

    a = {k: np.asarray(v) for k, v in inputs.items()}
    bf = ml_dtypes.bfloat16

    def by_feature(w):
        return w.reshape(PAIRS, 2, DK, D).transpose(3, 2, 1, 0).reshape(D, D)

    select = np.zeros((PARTS, E, NI - 1, 2, I), bf)
    for i in range(NI - 1):
        for j in range(2):
            select[:, 2 * i + j, i, j, :] = 1
    arrays = {
        "x": a["x"].reshape(T, D),
        "ctxT": a["ctx_1024"].reshape(T, D).T,
        "wqT": by_feature(a["L0_xattn_w_q"]),
        "wkT": by_feature(a["L0_xattn_w_k"]),
        "wvT": a["L0_xattn_w_v"].T,
        "woT": a["L0_xattn_w_o"].T,
        "bo": a["L0_xattn_b_o"],
        "maskq": a["mask_BxSxS2_ik0"],
        "maskT": a["mask_BxSxS2_ik0"].transpose(0, 2, 1),
        "gwT": a["L0_ffn_gate_w"].T,
        "gbias": a["L0_ffn_gate_bias"],
        "wgT": np.concatenate([a["L0_ffn_expert_gate"].reshape(E * I, D), a["L0_ffn_shared_gate"]]).T,
        "wuT": np.concatenate([a["L0_ffn_expert_up"].reshape(E * I, D), a["L0_ffn_shared_up"]]).T,
        "wdT": np.concatenate([a["L0_ffn_expert_down"].transpose(0, 2, 1).reshape(E * I, D),
                               a["L0_ffn_shared_down"].T]),
        "ident": np.eye(P, dtype=np.float32),
        "identb": np.eye(P).astype(bf),
        "sel": select.reshape(PARTS * E, (NI - 1) * P),
        "ones": np.ones((PARTS, PAIRS * T), bf),
    }
    arrays = {f"in_{k}": np.ascontiguousarray(v) for k, v in arrays.items()}
    nc = bacc.Bacc("TRN2", target_bir_lowering=False, num_devices=1)
    args = [nc.dram_tensor(k, v.shape, mybir.dt.from_np(v.dtype), kind="ExternalInput").ap()
            for k, v in arrays.items()]
    scratch = [nc.dram_tensor("qk_blocks", [BLOCKS, P, 2, T], BF16, kind="Internal").ap(),
               nc.dram_tensor("maxima", [B, PARTS * H, S], BF16, kind="Internal").ap()]
    out = nc.dram_tensor(_OUT, [D, T], F32, kind="ExternalOutput").ap()
    build(nc, *args, *scratch, out)
    r = run_bass_kernel_spmd(nc, [arrays], core_ids=[0])
    return r.results[0][_OUT].T.reshape(B, S, D)
```

```python
from contextlib import ExitStack

import numpy as np

import concourse.bass as bass
from concourse import mybir

F32 = mybir.dt.float32
F32R = mybir.dt.float32r
BF16 = mybir.dt.bfloat16
I32 = mybir.dt.int32
ALU = mybir.AluOpType
ACT = mybir.ActivationFunctionType
AX = mybir.AxisListType

P = 128
B, S, D = 4, 256, 128
H, DK = 16, 8
T = B * S
NC = T // P
QC = S // P
PAIRS = H // 2
PARTS = 3
BLOCKS = 6
STACK = BLOCKS * DK
STACKM = STACK + PARTS
HALFP = P // 2
VW = 32
VSLOT = VW // 2
E, I = 32, 64
NG, GE = 4, 8
TOPK = 8
FF = E * I + 2 * I
NI = FF // P
HALF = T // 2
HC = HALF // P
MASKED = -float(2**30)
QSCALE = float(1.0 / np.sqrt(np.float32(DK)))
EPS = 1e-5
ROUTED_SCALING = 2.5
FILL = -3.0e38
TAKEN = 3.0e38
PART_RING = 4
WB_RING = 3
LAG = 3
PIECES = 4
AHEAD = 12

KSPANS = [(0, S), (S, S), (2 * S, 2 * S)]
QSPANS = [(b * S, S) for b in range(B)]


def build(nc, x, ctxT, wqT, wkT, wvT, woT, bo, maskq, maskT, gwT, gbias, wgT, wuT, wdT,
          ident, identb, ones, qk_dram, m_dram, w_dram, outT):
    with ExitStack() as ctx:
        def sb(name, shape, dt):
            return ctx.enter_context(nc.sbuf_tensor(name, shape, dt))

        def sb_twice(first, then):
            with ExitStack() as early:
                before = [early.enter_context(nc.sbuf_tensor(*t)) for t in first]
            return before, [sb(*t) for t in then]

        def psum(name, shape, dt=F32):
            return ctx.enter_context(nc.psum_tensor(name, shape, dt))

        def sem(name):
            return ctx.enter_context(nc.semaphore(name))

        x_sb = sb("x_sb", [P, NC, D], F32)
        xb_sb = x_sb
        bo_sb = sb("bo_sb", [P, D], F32)
        wo_sb = sb("wo_sb", [P, P], F32)
        id_sb = sb("id_sb", [P, P], F32)
        idb_sb = sb("idb_sb", [P, P], BF16)
        m_sb = sb("m_sb", [P, 2, B, QC, S], I32)
        mq_sb, mt_sb = m_sb[:, 0], m_sb[:, 1]
        biasq = sb("biasq", [P, B, QC, S], BF16)
        biast = sb("biast", [P, B, QC, S], BF16)
        top_bias = sb("top_bias", [P, NC], F32)
        any_key = sb("any_key", [P, NC], F32)
        stats = sb("stats", [P, NC, 6], F32)
        mean_var = sb("mean_var", [P, NC, 2], F32)
        vareps = sb("vareps", [P, NC], F32)
        rstd = sb("rstd", [P, NC], F32)
        rs = sb("rs", [P, NC], F32)
        minus_half = sb("minus_half", [P, NC], F32)
        xn = sb("xn", [P, NC, D], F32)
        xnT = sb("xnT", [P, T], F32)
        stack = sb("stack", [P, PAIRS, 2, T], BF16)
        vs = sb("vs", [P, NC, H, VW], F32)

        def vs_of(u):
            return vs[:, :, :, :].rearrange("p c (g u j) w -> p (c g) u j w", u=2, j=4)[:, :, u]

        top = sb("top", [P, B, QC, H], F32)
        top_rest = sb("top_rest", [P, QC, H], F32)
        ntop = sb("ntop", [P, QC, PARTS, H], BF16)
        ntopT = sb("ntopT", [PARTS * H, 2, S], BF16)
        (prob,), (gate, gu, hid, hidh, hidl) = sb_twice(
            [("prob", [P, 4, 2, QC, S], F32)],
            [("gate", [P, 3, HALF], F32), ("gu", [P, 2, HALF], F32), ("hid", [P, 3, HALF], F32),
             ("hidh", [P, PART_RING, HALF], F32R), ("hidl", [P, PART_RING, HALF], F32R)])
        (ctxT_sb, qp, kp, rest_q, rest_k, wq_sb, wk_sb, wv_sb), (wdh, wdl, eneg, wfin) = sb_twice(
            [("ctxT_sb", [P, T], F32), ("qp", [P, PARTS, T], BF16), ("kp", [P, PARTS, T], BF16),
             ("rest_q", [P, 2, S], F32), ("rest_k", [P, HALF], F32),
             ("wq_sb", [P, P], F32), ("wk_sb", [P, P], F32), ("wv_sb", [P, P], F32)],
            [("wdh", [P, NI, D], F32R), ("wdl", [P, NI, D], F32R), ("eneg", [P, T], F32),
             ("wfin", [P, HC, E], F32)])
        oT = sb("oT", [P, 2, S], F32)
        zinv = sb("zinv", [P, QC, H // 2], F32)
        o_sb = sb("o_sb", [P, NC, D], F32)
        onT = sb("onT", [P, S], F32)
        stats2 = sb("stats2", [P, NC, 6], F32)
        mean_var2 = sb("mean_var2", [P, NC, 2], F32)
        vareps2 = sb("vareps2", [P, NC], F32)
        rstd2 = sb("rstd2", [P, NC], F32)
        xn2 = xn
        x1 = xnT[:, :].rearrange("p (c d) -> p c d", d=D)
        xh = sb("xh", [P, T], F32R)
        xl = sb("xl", [P, T], F32R)
        gw_sb = sb("gw_sb", [P, E], F32)
        gwh = sb("gwh", [P, E], F32R)
        gwl = sb("gwl", [P, E], F32R)
        gb_sb = sb("gb_sb", [P, E], F32)
        w_sb = sb("w_sb", [P, FF], F32)
        wgh = sb("wgh", [P, FF], F32R)
        wgl = sb("wgl", [P, FF], F32R)
        wuh = sb("wuh", [P, FF], F32R)
        wul = sb("wul", [P, FF], F32R)
        m_flat = m_sb[:, :, :, :, :].rearrange("p a b c k -> p (a b c k)")
        wd_sb = m_flat[:, 0:FF].bitcast(F32).rearrange("p (c d) -> p c d", d=D)
        wb_sb = m_flat[:, FF:FF + WB_RING * HALF].bitcast(F32).rearrange("p (n t) -> p n t", n=WB_RING)
        score = sb("score", [P, HC, E], F32)
        choice = sb("choice", [P, HC, E], F32)
        gtop = sb("gtop", [P, HC, NG, 8], F32)
        gscore = sb("gscore", [P, HC, 10], F32)
        gbest = sb("gbest", [P, HC, 8], F32)
        gtake = sb("gtake", [P, HC, 8], F32)
        gleft = sb("gleft", [P, HC, 10], F32)
        gmask = sb("gmask", [P, HC, NG], F32)
        cmask = sb("cmask", [P, HC, E], F32)
        ebest = sb("ebest", [P, HC, 8], F32)
        eleft = sb("eleft", [P, HC, E], F32)
        wsel = sb("wsel", [P, HC, E], F32)
        wsum = sb("wsum", [P, HC], F32)
        winv = sb("winv", [P, HC], F32)
        w_rows = eneg
        yT = x_sb[:, :, :].rearrange("p c d -> p (c d)")

        s_ps = psum("s_ps", [P, 4, 512])
        t_ps = psum("t_ps", [P, 2, 512])
        o_ps = psum("o_ps", [P, 512])
        m_ps = psum("m_ps", [P, 512])
        m_psb = m_ps[:, :].bitcast(BF16)

        d_xrest, d_ctxrest = sem("loaded_x_rest"), sem("loaded_ctx_rest")
        d_x, d_wq, d_wk, d_wv, d_wo = (sem(f"loaded_{n}") for n in ("x", "wq", "wk", "wv", "wo"))
        d_ctx, d_id, d_idb, d_bo = (sem(f"loaded_{n}") for n in ("ctx", "ident", "identb", "bo"))
        d_mq = [sem(f"loaded_maskq{b}") for b in range(B)]
        d_mt = [sem(f"loaded_maskT{b}") for b in range(B)]
        d_gw, d_gb, d_wg, d_wu, d_wd, d_ones = (sem(f"loaded_{n}") for n in ("gw", "gb", "wg", "wu", "wd", "ones"))
        q_out = [sem(f"q_parts_in_dram{b}") for b in range(B)]
        k_out = [sem(f"k_parts_in_dram{i}") for i in range(len(KSPANS))]
        stack_in = [sem(f"stacks_loaded{b}") for b in range(B)]
        m_out = [sem(f"maxima_in_dram{b}") for b in range(B)]
        m_in = [sem(f"maxima_loaded{b}") for b in range(B)]
        pool_set = sem("pool_set")
        bo_added = sem("bo_added")
        biasq_ready = sem("biasq_ready")
        biast_ready = sem("biast_ready")
        var_ready = sem("var_ready")
        rstd_ready = sem("rstd_ready")
        xn_ready = sem("xn_ready")
        xnT_ps = sem("xnT_ps")
        xnT_ready = sem("xnT_ready")
        k_ps, q_ps = sem("k_ps"), sem("q_ps")
        k_high, q_high = sem("k_high"), sem("q_high")
        k_rest, q_rest = sem("k_rest"), sem("q_rest")
        k_low, q_low = sem("k_low"), sem("q_low")
        v_ps = sem("v_ps")
        v_ready = sem("v_ready")
        dve_step = sem("dve_step")
        s_ready = sem("s_ready")
        top_ready = sem("top_ready")
        ntop_ready = sem("ntop_ready")
        ntopT_ready = sem("ntopT_ready")
        t_ready = sem("t_ready")
        p_ready = sem("p_ready")
        pv_done = sem("pv_done")
        oT_ready = sem("oT_ready")
        m_written = sem("m_written")
        m_read = sem("m_read")
        o_ready = sem("o_ready")
        onT_ready = sem("onT_ready")
        x1_ready = sem("x1_ready")
        var2_ready = sem("var2_ready")
        rstd2_ready = sem("rstd2_ready")
        xn2_ready = sem("xn2_ready")
        xh_ready, xl_ready = sem("xh_ready"), sem("xl_ready")
        w_rounded = sem("w_rounded")
        w_split = sem("w_split")
        gw_split = sem("gw_split")
        eneg_ready = sem("eneg_ready")
        wfin_ready = sem("wfin_ready")
        w_rows_ready = sem("w_rows_ready")
        w_out = [sem(f"routing_in_dram{f}") for f in range(2)]
        wb_in = [sem(f"routing_loaded{n}") for n in range(WB_RING)]
        g_ready, u_ready = sem("g_ready"), sem("u_ready")
        gate_ready = sem("gate_ready")
        gu_ready = sem("gu_ready")
        hid_ready, hidh_ready, hidl_ready = sem("hid_ready"), sem("hidh_ready"), sem("hidl_ready")
        wd_split = sem("wd_split")
        down_done = sem("down_done")
        yT_ready = sem("yT_ready")
        stored = sem("stored")

        uses = [("xnT", 0), ("xnT", 1), ("ntop", 0), ("xnT", 2), ("xnT", 3)]
        for b in range(B):
            if b == B - 1:
                uses += [("eneg", 0)]
            if b >= 1:
                uses += [("o", b - 1, 1), ("on", b - 1), ("proj", b - 1)]
            if b + 1 < B:
                uses += [("ntop", b + 1)]
            uses += [("o", b, 0)]
            if b == B - 1:
                uses += [("wT", 0)]
            if b >= 1:
                uses += [("xn2T", b - 1), ("logit", b - 1)]
        uses += [("o", B - 1, 1), ("on", B - 1), ("proj", B - 1), ("xn2T", B - 1), ("logit", B - 1),
                 ("eneg", 1), ("wT", 1)]

        def use(*key):
            return uses.index(tuple(key))

        pair_col = [(b, p) for b in range(B) for p in range(PAIRS)]
        NP = len(pair_col)

        def chunk_of(k):
            f, i = divmod(k, NI)
            c = (i - f) % NI
            return f, c, (f * (NI - 1) + c if c < NI - 1 else None)

        LAST = NP - AHEAD

        def t_bank(n, j):
            place = (n - LAST) % 3 if n >= LAST else 2
            return t_ps[:, j, :] if place == 2 else s_ps[:, 2 * place + j, :]

        def masked_by_pe(n):
            if n < AHEAD:
                return 2
            return 1 if n % 2 == 0 else 0

        def gu_bank(r, k):
            return s_ps[:, 2 * r + k % 3, :] if k % 3 < 2 else t_ps[:, r, :]

        step_of = {chunk_of(k)[2]: k for k in range(2 * NI)}

        def span_of(b):
            return min(b, len(KSPANS) - 1)

        def k_place(i):
            return t_ps[:, 0, 0:KSPANS[i][1]]

        def q_place(b):
            return t_ps[:, 1, 0:S] if b < B - 1 else o_ps[:, 0:S]

        block = ctx.enter_context(nc.Block())

        @block.sync
        def _(sp):
            xv = x.rearrange("(c p) d -> p c d", p=P)
            sp.dma_start(x_sb[:, 0:QC, :], xv[:, 0:QC, :]).then_inc(d_x, 16)
            sp.dma_start(mq_sb[:, 0, :, :], maskq[0].rearrange("(c p) k -> p c k", p=P)).then_inc(d_mq[0], 16)
            sp.dma_start(wk_sb[:, :], wkT).then_inc(d_wk, 16)
            sp.dma_start(ctxT_sb[:, 0:S], ctxT[:, 0:S]).then_inc(d_ctx, 16)
            sp.dma_start(id_sb[:, :], ident).then_inc(d_id, 16)
            sp.dma_start(wq_sb[:, :], wqT).then_inc(d_wq, 16)
            sp.dma_start(x_sb[:, QC:NC, :], xv[:, QC:NC, :]).then_inc(d_xrest, 16)

            def to_dram(which, parts, span, part, count, block, times, out):
                t0, n = span
                src = parts[:, part:part + count, t0:t0 + n]
                if times > 1:
                    src = src.broadcast_to([P, times, n])
                sp.dma_start(qk_dram[block:block + count * times, :, which, t0:t0 + n].rearrange("c r t -> r c t"),
                             src).then_inc(out, 16)

            def k_to_dram(i):
                sp.wait_ge(k_low, i + 1)
                for block, count in ((0, 3), (3, 2), (5, 1)):
                    to_dram(1, kp, KSPANS[i], 0, count, block, 1, k_out[i])

            def q_to_dram(i):
                sp.wait_ge(q_high, 2 * i + 1)
                to_dram(0, qp, QSPANS[i], 0, 1, 0, 3, q_out[i])
                sp.wait_ge(q_high, 2 * i + 2)
                to_dram(0, qp, QSPANS[i], 1, 1, 3, 2, q_out[i])
                sp.wait_ge(q_low, i + 1)
                to_dram(0, qp, QSPANS[i], 2, 1, 5, 1, q_out[i])

            def stacks_back(b):
                t0, n = QSPANS[b]
                sp.wait_ge(k_out[span_of(b)], 48)
                sp.wait_ge(q_out[b], 48)
                src = qk_dram.rearrange("c (d j p) w t -> j (c d) (p w) t", d=DK, j=2)
                for j in range(2):
                    sp.dma_start(stack[HALFP * j:HALFP * j + STACK, :, :, t0:t0 + n].rearrange("r p w t -> r (p w) t"),
                                 src[j, :, :, t0:t0 + n]).then_inc(stack_in[b], 16)

            sp.dma_start(wv_sb[:, :], wvT).then_inc(d_wv, 16)
            sp.dma_start(idb_sb[:, :], identb).then_inc(d_idb, 16)
            k_to_dram(0)
            sp.dma_start(ctxT_sb[:, S:T], ctxT[:, S:T]).then_inc(d_ctxrest, 16)
            sp.dma_start(mq_sb[:, 1, :, :], maskq[1].rearrange("(c p) k -> p c k", p=P)).then_inc(d_mq[1], 16)
            q_to_dram(0)
            stacks_back(0)
            k_to_dram(1)
            q_to_dram(1)
            stacks_back(1)
            for b in range(B):
                sp.wait_ge(ntopT_ready, b + 1)
                sp.dma_start(m_dram[b], ntopT[:, b % 2, :]).then_inc(m_out[b], 16)
                sp.wait_ge(m_out[b], 16)
                src = m_dram[b].rearrange("(c p j) t -> j c p t", c=PARTS, j=2)
                for j in range(2):
                    sp.dma_start(stack[HALFP * j + STACK:HALFP * j + STACKM, :, 0, b * S:(b + 1) * S],
                                 src[j]).then_inc(m_in[b], 16)
                if b == 0:
                    k_to_dram(2)
                    for late in range(2, B):
                        q_to_dram(late)
                        stacks_back(late)
            def store(f):
                sp.wait_ge(yT_ready, f + 1)
                sp.dma_start(outT[:, f * HALF:(f + 1) * HALF], yT[:, f * HALF:(f + 1) * HALF]).then_inc(stored, 16)

            sp.wait_ge(biasq_ready, B)
            sp.wait_ge(biast_ready, B)
            for f in range(2):
                sp.wait_ge(w_rows_ready, f + 1)
                sp.dma_start(w_dram[f], w_rows[0:E, f * HALF:(f + 1) * HALF]).then_inc(w_out[f], 16)
                sp.wait_ge(w_out[f], 16)
                for c in range(NI - 1):
                    n = f * (NI - 1) + c
                    if n >= WB_RING:
                        sp.wait_ge(hid_ready, step_of[n - WB_RING] + 1)
                    if (f, c) == (1, 6):
                        store(0)
                    sp.dma_start(wb_sb[:, n % WB_RING, :],
                                 w_dram[f, 2 * c:2 * c + 2, :].unsqueeze(1).broadcast_to([2, I, HALF])
                                 ).then_inc(wb_in[n % WB_RING], 16)
            store(1)
            sp.wait_ge(stored, 32)

        @block.gpsimd
        def _(pool):
            nc.gpsimd.memset(minus_half[:, :], -0.5).then_inc(pool_set, 1)
            pool.wait_ge(pool_set, 1)

            for n, (a, e) in enumerate(((0, QC), (QC, NC))):
                pool.wait_ge(var_ready, n + 1)
                nc.gpsimd.tensor_tensor(rstd[:, a:e], vareps[:, a:e], minus_half[:, a:e], ALU.pow).then_inc(rstd_ready, 1)
            for u in range(2):
                v, ones_at = vs_of(u), u * VSLOT + DK
                if u:
                    nc.gpsimd.memset(v[:, :, :, 0:VSLOT], 0.0)
                nc.gpsimd.memset(v[:, :, :, ones_at:ones_at + 1], 1.0)
                nc.gpsimd.memset(v[:, :, :, ones_at + 1:VW], 0.0)
            nc.gpsimd.memset(gscore[:, :, NG:10], FILL)
            nc.gpsimd.memset(gtake[:, :, 2:8], FILL).then_inc(pool_set, 1)
            pool.wait_ge(biasq_ready, 2)
            for b in range(2, B):
                pool.wait_ge(d_mq[b], 16)
                nc.gpsimd.tensor_scalar(biasq[:, b, :, :], mq_sb[:, b, :, :], 0.0, MASKED,
                                        ALU.is_equal, ALU.mult).then_inc(biasq_ready, 1)
            pool.dma_start(w_sb[:, :], wgT).then_inc(d_wg, 16)
            for b in range(B):
                pool.wait_ge(d_mt[b], 16)
                nc.gpsimd.tensor_scalar(biast[:, b, :, :], mt_sb[:, b, :, :], 0.0, MASKED,
                                        ALU.is_equal, ALU.mult).then_inc(biast_ready, 1)
            pool.dma_start(bo_sb[:, :], bo.partition_broadcast(P)).then_inc(d_bo, 16)
            pool.dma_start(wo_sb[:, :], woT).then_inc(d_wo, 16)
            pool.dma_start(gw_sb[:, :], gwT).then_inc(d_gw, 16)
            pool.dma_start(gb_sb[:, :], gbias.partition_broadcast(P)).then_inc(d_gb, 16)
            pool.wait_ge(d_bo, 16)
            pool.wait_ge(xn_ready, NC)
            for c in range(NC):
                last = nc.gpsimd.tensor_tensor(xb_sb[:, c, :], x_sb[:, c, :], bo_sb[:, :], ALU.add)
            last.then_inc(bo_added, 1)
            pool.wait_ge(d_gw, 16)
            nc.gpsimd.tensor_copy(gwh[:, :], gw_sb[:, :]).then_inc(gw_split, 1)
            pool.wait_ge(gw_split, 1)
            nc.gpsimd.tensor_tensor(gwl[:, :], gw_sb[:, :], gwh[:, :].bitcast(F32), ALU.subtract).then_inc(gw_split, 1)

            def rstd2_step(b):
                pool.wait_ge(var2_ready, b + 1)
                cs = slice(QC * b, QC * b + QC)
                nc.gpsimd.tensor_tensor(rstd2[:, cs], vareps2[:, cs], minus_half[:, cs], ALU.pow).then_inc(rstd2_ready, 1)

            for r, (hi, lo) in enumerate(((wgh, wgl), (wuh, wul))):
                pool.wait_ge(w_rounded, PIECES * (r + 1))
                nc.gpsimd.tensor_tensor(lo[:, :], w_sb[:, :], hi[:, :].bitcast(F32), ALU.subtract).then_inc(w_split, 1)
                if r == 0:
                    pool.wait_ge(m_in[1], 32)
                    pool.wait_ge(w_split, 1)
                    pool.dma_start(w_sb[:, :], wuT).then_inc(d_wu, 16)
                    pool.wait_ge(biasq_ready, B)
                    pool.wait_ge(biast_ready, B)
                    pool.dma_start(wd_sb[:, :, :], wdT.rearrange("(c p) d -> p c d", p=P)).then_inc(d_wd, 16)
                    rstd2_step(0)
            rstd2_step(1)
            pool.wait_ge(wd_split, PIECES)
            nc.gpsimd.tensor_tensor(wdl[:, :, :], wd_sb[:, :, :], wdh[:, :, :].bitcast(F32),
                                    ALU.subtract).then_inc(wd_split, 1)
            rstd2_step(2)
            for k in range(2 * NI):
                if k == 5:
                    rstd2_step(3)
                pool.wait_ge(hidh_ready, k + 1)
                nc.gpsimd.tensor_tensor(hidl[:, k % PART_RING, :], hid[:, k % 3, :],
                                        hidh[:, k % PART_RING, :].bitcast(F32), ALU.subtract).then_inc(hidl_ready, 1)

        @block.tensor
        def _(pe):
            def m_use(*key):
                n = use(*key)
                if n:
                    pe.wait_ge(m_read, n)

            def k_proj(i):
                t0, n = KSPANS[i]
                if i:
                    pe.wait_ge(d_ctxrest, 16)
                    pe.wait_ge(k_rest, i)
                nc.tensor.matmul(k_place(i), wk_sb[:, :], ctxT_sb[:, t0:t0 + n],
                                 start=True, stop=True).then_inc(k_ps, 1)

            def x_transposes(i):
                t0, n = QSPANS[i]
                m_use("xnT", i)
                pe.wait_ge(xn_ready, (t0 + n) // P)
                for c in range(n // P):
                    last = nc.tensor.transpose(m_ps[:, c * P:(c + 1) * P], xn[:, t0 // P + c, :], id_sb[:, :])
                last.then_inc(m_written, 1)

            def q_proj(i):
                t0, n = QSPANS[i]
                pe.wait_ge(xnT_ready, i + 1)
                if i == B - 1:
                    pe.wait_ge(v_ready, 4)
                elif i:
                    pe.wait_ge(q_rest, i)
                nc.tensor.matmul(q_place(i), wq_sb[:, :], xnT[:, t0:t0 + n],
                                 start=True, stop=True).then_inc(q_ps, 1)

            def keep_warm(count):
                pe.wait_ge(v_ready, 4)
                for _ in range(count):
                    nc.tensor.matmul(o_ps[:, :], idb_sb[:, :], biasq[:, 0, :, :], start=True, stop=True)

            def v_proj(i):
                pe.wait_ge(v_ready if i else d_wv, 2 * i if i else 16)
                for c in range(4):
                    last = nc.tensor.matmul(o_ps[:, c * P:(c + 1) * P],
                                            ctxT_sb[:, (4 * i + c) * P:(4 * i + c + 1) * P], wv_sb[:, :],
                                            start=True, stop=True)
                last.then_inc(v_ps, 1)

            def scores(n):
                b, p = pair_col[n]
                t0 = b * S
                r = 2 * (n % 2)
                if n >= 2:
                    pe.wait_ge(top_ready, n - 1)
                if p == 0:
                    pe.wait_ge(biasq_ready, b + 1)
                    pe.wait_ge(stack_in[b], 32)
                heads = masked_by_pe(n)
                for j in range(heads):
                    nc.tensor.matmul(s_ps[:, r + j, :], idb_sb[:, :], biasq[:, b, :, :],
                                     start=True, stop=False, skip_group_check=True)
                for c in range(QC):
                    for j in range(2):
                        rows = slice(HALFP * j, HALFP * j + STACK)
                        last = nc.tensor.matmul(s_ps[:, r + j, c * S:(c + 1) * S],
                                                stack[rows, p, 0, t0 + c * P:t0 + (c + 1) * P],
                                                stack[rows, p, 1, t0:t0 + S],
                                                start=(j >= heads and c == 0), stop=True, skip_group_check=True)
                last.then_inc(s_ready, 1)

            def scores_t(n):
                b, p = pair_col[n]
                t0 = b * S
                if n == 0:
                    pe.wait_ge(k_rest, len(KSPANS))
                    pe.wait_ge(q_rest, B - 1)
                    pe.wait_ge(d_ones, 32)
                if p == 0:
                    pe.wait_ge(biast_ready, b + 1)
                    pe.wait_ge(m_in[b], 32)

                def mask(j):
                    if n >= LAST + 2:
                        pe.wait_ge(p_ready, 2 * (n - 3) + j + 1)
                    elif n >= LAST:
                        pe.wait_ge(top_ready, n - LAST + NP - 1)
                    elif n >= 1:
                        pe.wait_ge(p_ready, 2 * (n - 1) + j + 1)
                    nc.tensor.matmul(t_bank(n, j), idb_sb[:, :], biast[:, b, :, :],
                                     start=True, stop=False, skip_group_check=True)

                def product(j, c):
                    rows = slice(HALFP * j, HALFP * j + STACKM)
                    return nc.tensor.matmul(t_bank(n, j)[:, c * S:(c + 1) * S],
                                            stack[rows, p, 1, t0 + c * P:t0 + (c + 1) * P],
                                            stack[rows, p, 0, t0:t0 + S],
                                            start=False, stop=True, skip_group_check=True)

                if n + AHEAD < NP:
                    mask(0)
                    mask(1)
                    product(0, 0)
                    product(1, 0)
                    product(0, 1).then_inc(t_ready, 1)
                    product(1, 1).then_inc(t_ready, 1)
                else:
                    for j in range(2):
                        mask(j)
                        product(j, 0)
                        product(j, 1).then_inc(t_ready, 1)

            def pv(q):
                b, g, u = q // 4, q // 2 % 2, q % 2
                pe.wait_ge(p_ready, 4 * q + 4)
                if q == 0:
                    pe.wait_ge(v_ready, 4)
                    pe.wait_ge(q_rest, B)
                    pe.wait_ge(pool_set, 2)
                if b >= 1 and u == 0:
                    pe.wait_ge(oT_ready, 2 * (b - 1) + g + 1)
                for c in range(QC):
                    for j in range(4):
                        n = 2 * q + j // 2
                        last = nc.tensor.matmul(o_ps[VW * j:VW * (j + 1), g * S:(g + 1) * S],
                                                vs[:, QC * b + c, 8 * g + 4 * u + j, :],
                                                prob[:, n % 4, j % 2, c, :],
                                                start=(u == 0 and c == 0), stop=(u == 1 and c == QC - 1),
                                                skip_group_check=True)
                last.then_inc(pv_done, 1)

            def ntop_transpose(b):
                m_use("ntop", b)
                pe.wait_ge(ntop_ready, b + 1)
                for c in range(QC):
                    last = nc.tensor.transpose(m_psb[0:PARTS * H, c * P:(c + 1) * P], ntop[:, c, :, :], idb_sb[:, :])
                last.then_inc(m_written, 1)

            def o_transpose(b, half):
                m_use("o", b, half)
                pe.wait_ge(oT_ready, 2 * b + half + 1)
                for c in range(QC):
                    last = nc.tensor.transpose(m_ps[:, c * P:(c + 1) * P], oT[:, half, c * P:(c + 1) * P], id_sb[:, :])
                last.then_inc(m_written, 1)

            def on_transpose(b):
                m_use("on", b)
                pe.wait_ge(o_ready, 2 * b + 2)
                for c in range(QC):
                    last = nc.tensor.transpose(m_ps[:, c * P:(c + 1) * P], o_sb[:, QC * b + c, :], id_sb[:, :])
                last.then_inc(m_written, 1)

            def out_proj(b):
                m_use("proj", b)
                pe.wait_ge(onT_ready, b + 1)
                if b == 0:
                    pe.wait_ge(d_wo, 16)
                for c in range(QC):
                    last = nc.tensor.matmul(m_ps[:, c * P:(c + 1) * P], onT[:, c * P:(c + 1) * P], wo_sb[:, :],
                                            start=True, stop=True)
                last.then_inc(m_written, 1)

            def xn2_transpose(b):
                m_use("xn2T", b)
                pe.wait_ge(xn2_ready, b + 1)
                for c in range(QC):
                    last = nc.tensor.transpose(m_ps[:, c * P:(c + 1) * P], xn2[:, QC * b + c, :], id_sb[:, :])
                last.then_inc(m_written, 1)

            def logits(b):
                m_use("logit", b)
                pe.wait_ge(xl_ready, b + 1)
                if b == 0:
                    pe.wait_ge(gw_split, 2)
                t = slice(b * S, (b + 1) * S)
                out = m_ps[0:E, 0:S]
                nc.tensor.matmul(out, gwh[:, :], xh[:, t], start=True, stop=False)
                nc.tensor.matmul(out, gwh[:, :], xl[:, t], start=False, stop=False)
                nc.tensor.matmul(out, gwl[:, :], xh[:, t], start=False, stop=True).then_inc(m_written, 1)

            def eneg_transpose(f):
                m_use("eneg", f)
                pe.wait_ge(eneg_ready, 2 * f + 2)
                for c in range(HC):
                    last = nc.tensor.transpose(m_ps[:, c * E:(c + 1) * E],
                                               eneg[0:E, (HC * f + c) * P:(HC * f + c + 1) * P], id_sb[0:E, 0:E])
                last.then_inc(m_written, 1)

            def w_transpose(f):
                m_use("wT", f)
                pe.wait_ge(wfin_ready, f + 1)
                for c in range(HC):
                    last = nc.tensor.transpose(m_ps[0:E, c * P:(c + 1) * P], wfin[:, c, :], id_sb[:, :])
                last.then_inc(m_written, 1)

            def y_bank(f):
                return o_ps if f == 0 else m_ps

            def residual(f):
                if f == 0:
                    pe.wait_ge(oT_ready, 2 * B)
                else:
                    m_use("wT", 1)
                    pe.wait_ge(m_read, use("wT", 1) + 1)
                pe.wait_ge(x1_ready, 2 * f + 2)
                for c in range(HC):
                    nc.tensor.matmul(y_bank(f)[:, c * P:(c + 1) * P], x1[:, HC * f + c, :], id_sb[:, :],
                                     start=(c == 0), stop=False, skip_group_check=True)

            def gate_up(k):
                f, c, _ = chunk_of(k)
                t = slice(f * HALF, (f + 1) * HALF)
                w = slice(c * P, (c + 1) * P)
                if k % NI == 0:
                    pe.wait_ge(xl_ready, 2 * f + 2)
                if k == 0:
                    pe.wait_ge(w_split, 2)
                if k < 3:
                    pe.wait_ge(p_ready, (2 * (NP - 2) + 1, 2 * (NP - 1), 2 * NP)[k])
                for r, (hi, lo, ready, free) in enumerate(((wgh, wgl, g_ready, gate_ready),
                                                           (wuh, wul, u_ready, gu_ready))):
                    if k >= 3:
                        pe.wait_ge(free, k - 2)
                    out = gu_bank(r, k)
                    nc.tensor.matmul(out, hi[:, w], xh[:, t], start=True, stop=False)
                    nc.tensor.matmul(out, hi[:, w], xl[:, t], start=False, stop=False)
                    nc.tensor.matmul(out, lo[:, w], xh[:, t], start=False, stop=True).then_inc(ready, 1)

            def down(k):
                f, c, _ = chunk_of(k)
                pe.wait_ge(hidh_ready, k + 1)
                if k == 0:
                    pe.wait_ge(wd_split, PIECES + 1)
                out, h, l = y_bank(f)[:, :], hidh[:, k % PART_RING, :], hidl[:, k % PART_RING, :]
                nc.tensor.matmul(out, wdh[:, c, :], h, start=False, stop=False, skip_group_check=True)
                nc.tensor.matmul(out, wdl[:, c, :], h, start=False, stop=False, skip_group_check=True)
                pe.wait_ge(hidl_ready, k + 1)
                nc.tensor.matmul(out, wdh[:, c, :], l, start=False, stop=(k % NI == NI - 1),
                                 skip_group_check=True).then_inc(down_done, 1)

            pe.wait_ge(d_wk, 16)
            pe.wait_ge(d_ctx, 16)
            k_proj(0)
            pe.wait_ge(d_id, 16)
            x_transposes(0)
            pe.wait_ge(d_wq, 16)
            q_proj(0)
            k_proj(1)
            v_proj(0)
            x_transposes(1)
            k_proj(2)
            q_proj(1)
            pe.wait_ge(d_idb, 16)
            for n in range(AHEAD - 1):
                scores(n)
                if n == PAIRS + 1:
                    ntop_transpose(0)
                    v_proj(1)
                    x_transposes(2)
                    q_proj(2)
            keep_warm(12)
            x_transposes(3)
            keep_warm(4)
            q_proj(3)
            late = {0: (AHEAD - 1,), 1: (AHEAD,), 2: (AHEAD + 1, AHEAD + 2)}
            for n in range(NP):
                b, p = pair_col[n]
                if n not in late and n + AHEAD < NP:
                    scores(n + AHEAD)
                scores_t(n)
                for m in late.get(n, ()):
                    scores(m)
                if n >= 2 and n % 2 == 0:
                    pv(n // 2 - 1)
                if (b, p) == (B - 1, 0):
                    eneg_transpose(0)
                if b >= 1 and p == 1:
                    o_transpose(b - 1, 1)
                if b >= 1 and p == 2:
                    on_transpose(b - 1)
                if b >= 1 and p == 3:
                    out_proj(b - 1)
                if p == 4 and b + 1 < B:
                    ntop_transpose(b + 1)
                if p == 5:
                    o_transpose(b, 0)
                if (b, p) == (B - 1, 6):
                    w_transpose(0)
                if b >= 1 and p == 6:
                    xn2_transpose(b - 1)
                if b >= 1 and p == 7:
                    logits(b - 1)
            gate_up(0)
            pv(NP // 2 - 1)
            gate_up(1)
            residual(0)
            o_transpose(B - 1, 1)
            steps = {2: lambda: on_transpose(B - 1), 3: lambda: out_proj(B - 1),
                     6: lambda: xn2_transpose(B - 1), 7: lambda: logits(B - 1), 8: lambda: eneg_transpose(1),
                     NI - 1: lambda: w_transpose(1), NI: lambda: residual(1)}
            for k in range(2, 2 * NI + LAG):
                if k < 2 * NI:
                    gate_up(k)
                if k >= LAG:
                    down(k - LAG)
                if k in steps:
                    steps[k]()

        @block.scalar
        def _(act):
            def high_part(i, ps, place, span, parts, high, scale):
                t0, n = span
                act.wait_ge(ps, i + 1)
                nc.scalar.activation(parts[:, 0, t0:t0 + n], place, ACT.Copy, scale=scale).then_inc(high, 1)

            def mid_part(i, span, parts, high, rest_ready, rest):
                t0, n = span
                act.wait_ge(rest_ready, i + 1)
                nc.scalar.activation(parts[:, 1, t0:t0 + n], rest[:, 0:n], ACT.Copy).then_inc(high, 1)

            def v_copy(i):
                act.wait_ge(v_ps, i + 1)
                for u in range(2):
                    src = o_ps[:, :].rearrange("p (c u j d) -> p c u j d", u=2, j=4, d=DK)[:, :, u]
                    nc.scalar.activation(vs_of(u)[:, 8 * i:8 * i + 8, :, u * VSLOT:u * VSLOT + DK], src,
                                         ACT.Copy).then_inc(v_ready, 1)

            def xnT_copy(i):
                t0, n = QSPANS[i]
                act.wait_ge(m_written, use("xnT", i) + 1)
                nc.scalar.activation(xnT[:, t0:t0 + n], m_ps[:, 0:n], ACT.Copy).then_inc(m_read, 1)
                act.wait_ge(m_read, use("xnT", i) + 1)
                act.sem_inc(xnT_ready, 1)

            def ntopT_copy(b):
                act.wait_ge(m_written, use("ntop", b) + 1)
                if b >= 2:
                    act.wait_ge(m_out[b - 2], 16)
                nc.scalar.activation(ntopT[:, b % 2, :], m_psb[0:PARTS * H, 0:S], ACT.Copy).then_inc(m_read, 1)
                act.wait_ge(m_read, use("ntop", b) + 1)
                act.sem_inc(ntopT_ready, 1)

            def exp(n):
                if n >= 4:
                    act.wait_ge(pv_done, (n - 4) // 2 + 1)
                for j in range(2):
                    act.wait_ge(t_ready, 2 * n + j + 1)
                    nc.scalar.activation(prob[:, n % 4, j, :, :].rearrange("p c q -> p (c q)"), t_bank(n, j),
                                         ACT.Exp).then_inc(p_ready, 1)

            def oT_copy(h):
                act.wait_ge(pv_done, 2 * h + 2)
                if h >= 2:
                    act.wait_ge(m_written, use("o", h // 2 - 1, h % 2) + 1)
                nc.scalar.activation(oT[:, h % 2, :], o_ps[:, h % 2 * S:(h % 2 + 1) * S], ACT.Copy).then_inc(oT_ready, 1)

            def onT_copy(b):
                act.wait_ge(m_written, use("on", b) + 1)
                nc.scalar.activation(onT[:, :], m_ps[:, 0:S], ACT.Copy).then_inc(m_read, 1)
                act.wait_ge(m_read, use("on", b) + 1)
                act.sem_inc(onT_ready, 1)

            def xh_copy(b):
                act.wait_ge(m_written, use("xn2T", b) + 1)
                nc.scalar.activation(xh[:, b * S:(b + 1) * S], m_ps[:, 0:S], ACT.Copy).then_inc(xh_ready, 1)

            def eneg_step(b):
                act.wait_ge(m_written, use("logit", b) + 1)
                nc.scalar.activation(eneg[0:E, b * S:(b + 1) * S], m_ps[0:E, 0:S], ACT.Exp, scale=-1.0).then_inc(m_read, 1)
                act.wait_ge(m_read, use("logit", b) + 1)
                act.sem_inc(eneg_ready, 1)

            def w_rows_copy(f):
                act.wait_ge(m_written, use("wT", f) + 1)
                nc.scalar.activation(w_rows[0:E, f * HALF:(f + 1) * HALF], m_ps[0:E, 0:HALF], ACT.Copy).then_inc(m_read, 1)
                act.wait_ge(m_read, use("wT", f) + 1)
                act.sem_inc(w_rows_ready, 1)

            def w_high(r, i):
                if i == 0:
                    act.wait_ge((d_wg, d_wu)[r], 16)
                c = slice(i * FF // PIECES, (i + 1) * FF // PIECES)
                nc.scalar.activation((wgh, wuh)[r][:, c], w_sb[:, c], ACT.Copy).then_inc(w_rounded, 1)

            def silu(k):
                act.wait_ge(g_ready, k + 1)
                if k >= 3:
                    act.wait_ge(gu_ready, k - 2)
                nc.scalar.activation(gate[:, k % 3, :], gu_bank(0, k), ACT.Silu).then_inc(gate_ready, 1)

            def hidden_high(k):
                act.wait_ge(hid_ready, k + 1)
                if k >= PART_RING:
                    act.wait_ge(down_done, k - PART_RING + 1)
                nc.scalar.activation(hidh[:, k % PART_RING, :], hid[:, k % 3, :], ACT.Copy).then_inc(hidh_ready, 1)

            def wd_high(i):
                if i == 0:
                    for out in q_out + k_out:
                        act.wait_ge(out, 48)
                    act.wait_ge(v_ps, 2)
                    act.wait_ge(d_wd, 16)
                c = slice(i * FF // PIECES, (i + 1) * FF // PIECES)
                nc.scalar.activation(wdh[:, :, :].rearrange("p c d -> p (c d)")[:, c],
                                     wd_sb[:, :, :].rearrange("p c d -> p (c d)")[:, c], ACT.Copy).then_inc(wd_split, 1)

            def y_copy(f):
                act.wait_ge(down_done, (f + 1) * NI)
                bank = o_ps if f == 0 else m_ps
                nc.scalar.activation(yT[:, f * HALF:(f + 1) * HALF], bank[:, :], ACT.Copy).then_inc(yT_ready, 1)

            def k_high_part(i):
                high_part(i, k_ps, k_place(i), KSPANS[i], kp, k_high, 1.0)

            def k_mid_part(i):
                mid_part(i, KSPANS[i], kp, k_high, k_rest, rest_k)

            def q_high_part(i):
                high_part(i, q_ps, q_place(i), QSPANS[i], qp, q_high, QSCALE)

            def q_mid_part(i):
                mid_part(i, QSPANS[i], qp, q_high, q_rest, rest_q[:, i % 2, :])

            for i in range(2):
                k_high_part(i)
                k_mid_part(i)
                xnT_copy(i)
                q_high_part(i)
                q_mid_part(i)
            v_copy(0)
            k_high_part(2)
            act.wait_ge(stack_in[0], 32)
            for b in range(2, B):
                act.dma_start(mq_sb[:, b, :, :], maskq[b].rearrange("(c p) k -> p c k", p=P)).then_inc(d_mq[b], 16)
            for b in range(B):
                act.dma_start(mt_sb[:, b, :, :], maskT[b].rearrange("(c p) k -> p c k", p=P)).then_inc(d_mt[b], 16)
            for j in range(2):
                act.dma_start(stack[HALFP * j + STACK:HALFP * j + STACKM, :, 1, :],
                              ones.rearrange("c (p t) -> c p t", p=PAIRS)).then_inc(d_ones, 16)
            ntopT_copy(0)
            v_copy(1)
            xnT_copy(2)
            k_mid_part(2)
            q_high_part(2)
            q_mid_part(2)
            xnT_copy(3)
            q_high_part(3)
            q_mid_part(3)
            for n in range(NP):
                b, p = pair_col[n]
                exp(n)
                if n >= 4 and n % 4 == 0:
                    oT_copy(n // 4 - 1)
                if 2 <= n < 2 + PIECES:
                    w_high(0, n - 2)
                if 12 <= n < 12 + PIECES:
                    w_high(1, n - 12)
                if 16 <= n < 16 + PIECES:
                    wd_high(n - 16)
                if b >= 1 and p == 2:
                    onT_copy(b - 1)
                if p == 4 and b + 1 < B:
                    ntopT_copy(b + 1)
                if (b, p) == (B - 1, 6):
                    w_rows_copy(0)
                if b >= 1 and p == 6:
                    xh_copy(b - 1)
                if b >= 1 and p == 7:
                    eneg_step(b - 1)
            silu(0)
            oT_copy(NP // 4 - 1)
            steps = {2: lambda: onT_copy(B - 1), 6: lambda: xh_copy(B - 1), 7: lambda: eneg_step(B - 1),
                     NI - 1: lambda: w_rows_copy(1)}
            steps[NI + LAG] = lambda: y_copy(0)
            for k in range(1, 2 * NI + 1):
                if k < 2 * NI:
                    silu(k)
                hidden_high(k - 1)
                if k in steps:
                    steps[k]()
            y_copy(1)

        @block.vector
        def _(dve):
            chain = [0]

            def link(ins):
                chain[0] += 1
                ins.then_inc(dve_step, 1)
                dve.wait_ge(dve_step, chain[0])

            def bias_q(b):
                dve.wait_ge(d_mq[b], 16)
                link(nc.vector.tensor_scalar(biasq[:, b, :, :], mq_sb[:, b, :, :], 0.0, MASKED,
                                             ALU.is_equal, ALU.mult))
                dve.sem_inc(biasq_ready, 1)

            def keys_left(b):
                if b >= 2:
                    dve.wait_ge(biasq_ready, b + 1)
                cs = slice(QC * b, QC * b + QC)
                link(nc.vector.tensor_reduce(top_bias[:, cs], biasq[:, b, :, :], AX.X, ALU.max))
                link(nc.vector.tensor_scalar(any_key[:, cs], top_bias[:, cs], MASKED, None, ALU.is_gt))

            def moments(a, e, src, st, mv, ve, ready):
                for c in range(a, e):
                    last = nc.vector.bn_stats(st[:, c, :], src[:, c, :])
                link(last)
                for c in range(a, e):
                    last = nc.vector.bn_aggr(mv[:, c, :], st[:, c, :])
                link(last)
                nc.vector.tensor_scalar(ve[:, a:e], mv[:, a:e, 1], EPS, None, ALU.add).then_inc(ready, 1)

            def normalise(i):
                a, e = QSPANS[i][0] // P, sum(QSPANS[i]) // P
                dve.wait_ge(rstd_ready, min(i, 1) + 1)
                link(nc.vector.tensor_tensor(rs[:, a:e], rstd[:, a:e], any_key[:, a:e], ALU.mult))
                for c in range(a, e):
                    nc.vector.tensor_scalar(xn[:, c, :], x_sb[:, c, :], mean_var[:, c, 0:1], rs[:, c:c + 1],
                                            ALU.subtract, ALU.mult).then_inc(xn_ready, 1)

            def rest_step(i, place, span, parts, high, rest_ready, rest, scale):
                t0, n = span
                dve.wait_ge(high, 2 * i + 1)
                nc.vector.scalar_tensor_tensor(out=rest[:, 0:n], in0=place, scalar=scale,
                                               in1=parts[:, 0, t0:t0 + n], op0=ALU.mult,
                                               op1=ALU.subtract).then_inc(rest_ready, 1)

            def low_step(i, span, parts, high, rest_ready, rest, low):
                t0, n = span
                dve.wait_ge(high, 2 * i + 2)
                dve.wait_ge(rest_ready, i + 1)
                nc.vector.tensor_tensor(parts[:, 2, t0:t0 + n], rest[:, 0:n], parts[:, 1, t0:t0 + n],
                                        ALU.subtract).then_inc(low, 1)

            def row_max(n):
                b, p = pair_col[n]
                r = 2 * (n % 2)
                dve.wait_ge(s_ready, n + 1)
                heads = masked_by_pe(n)
                for j in range(heads, 2):
                    for c in range(QC):
                        scores = s_ps[:, r + j, c * S:(c + 1) * S]
                        last = nc.vector.tensor_tensor_reduce(
                            scores, scores, biasq[:, b, c, :],
                            1.0, -3.0e38, ALU.add, ALU.max, top[:, b, c, 2 * p + j:2 * p + j + 1])
                if heads:
                    last = nc.vector.tensor_reduce(top[:, b, :, 2 * p:2 * p + heads].rearrange("q c j -> q j c"),
                                                   s_ps[:, r:r + heads, :].rearrange("q j (c k) -> q j c k", c=QC),
                                                   AX.X, ALU.max)
                last.then_inc(top_ready, 1)

            def minus_top(b):
                dve.wait_ge(top_ready, PAIRS * (b + 1))
                if b >= 1:
                    dve.wait_ge(m_written, use("ntop", b - 1) + 1)
                link(nc.vector.tensor_scalar(ntop[:, :, 0, :], top[:, b, :, :], -1.0, None, ALU.mult))
                link(nc.vector.scalar_tensor_tensor(out=top_rest[:, :, :], in0=top[:, b, :, :], scalar=-1.0,
                                                    in1=ntop[:, :, 0, :], op0=ALU.mult, op1=ALU.subtract))
                link(nc.vector.tensor_copy(ntop[:, :, 1, :], top_rest[:, :, :]))
                nc.vector.tensor_tensor(ntop[:, :, 2, :], top_rest[:, :, :], ntop[:, :, 1, :],
                                        ALU.subtract).then_inc(ntop_ready, 1)

            def divide(b, half):
                n = use("o", b, half)
                dve.wait_ge(m_written, n + 1)
                src = m_ps[:, 0:S].rearrange("q (c h w) -> q c h w", c=QC, w=VSLOT)
                link(nc.vector.reciprocal(zinv[:, :, :], src[:, :, :, DK]))
                dst = o_sb[:, QC * b:QC * b + QC, half * D // 2:(half + 1) * D // 2]
                link(nc.vector.tensor_tensor(dst.rearrange("q c (h d) -> q c h d", d=DK), src[:, :, :, 0:DK],
                                             zinv[:, :, :].unsqueeze(3).broadcast_to([P, QC, H // 2, DK]), ALU.mult))
                dve.sem_inc(m_read, 1)
                dve.sem_inc(o_ready, 1)

            def x1_add(b):
                dve.wait_ge(m_written, use("proj", b) + 1)
                if b == 0:
                    dve.wait_ge(bo_added, 1)
                cs = slice(QC * b, QC * b + QC)
                link(nc.vector.tensor_tensor(x1[:, cs, :], m_ps[:, 0:S].rearrange("p (c d) -> p c d", c=QC),
                                             xb_sb[:, cs, :], ALU.add))
                dve.sem_inc(m_read, 1)
                dve.sem_inc(x1_ready, 1)

            def x1_moments(b):
                moments(QC * b, QC * b + QC, x1, stats2, mean_var2, vareps2, var2_ready)

            def normalise2(b):
                dve.wait_ge(rstd2_ready, b + 1)
                for c in range(QC * b, QC * b + QC):
                    last = nc.vector.tensor_scalar(xn2[:, c, :], x1[:, c, :], mean_var2[:, c, 0:1],
                                                   rstd2[:, c:c + 1], ALU.subtract, ALU.mult)
                last.then_inc(xn2_ready, 1)

            def xl_step(b):
                dve.wait_ge(xh_ready, b + 1)
                t = slice(b * S, (b + 1) * S)
                link(nc.vector.tensor_tensor(xl[:, t], m_ps[:, 0:S], xh[:, t].bitcast(F32), ALU.subtract))
                dve.sem_inc(m_read, 1)
                dve.sem_inc(xl_ready, 1)

            def routing(f):
                cs = slice(0, HC)
                chunks = range(HC)

                def scores_step():
                    dve.wait_ge(m_written, use("eneg", f) + 1)
                    if f == 0:
                        dve.wait_ge(d_gb, 16)
                        dve.wait_ge(pool_set, 2)
                    link(nc.vector.tensor_scalar(wfin[:, cs, :], m_ps[:, 0:HC * E].rearrange("p (c e) -> p c e", c=HC),
                                                 1.0, None, ALU.add))
                    dve.sem_inc(m_read, 1)
                    link(nc.vector.reciprocal(score[:, cs, :], wfin[:, cs, :]))
                    link(nc.vector.tensor_tensor(choice[:, cs, :], score[:, cs, :],
                                                 gb_sb[:, :].unsqueeze(1).broadcast_to([P, HC, E]), ALU.add))

                def best_of_groups():
                    for c in chunks:
                        for g in range(NG):
                            last = nc.vector.max(gtop[:, c, g, :], choice[:, c, g * GE:(g + 1) * GE])
                    link(last)

                def group_scores():
                    link(nc.vector.tensor_tensor(gscore[:, cs, 0:NG], gtop[:, cs, :, 0], gtop[:, cs, :, 1], ALU.add))
                    for c in chunks:
                        last = nc.vector.max(gbest[:, c, :], gscore[:, c, :])
                    link(last)
                    link(nc.vector.tensor_copy(gtake[:, cs, 0:2], gbest[:, cs, 0:2]))

                def chosen_groups():
                    for c in chunks:
                        last = nc.vector.match_replace(gleft[:, c, :], gtake[:, c, :], gscore[:, c, :], TAKEN)
                    link(last)
                    link(nc.vector.tensor_scalar(gmask[:, cs, :], gleft[:, cs, 0:NG], TAKEN, None, ALU.is_equal))
                    link(nc.vector.tensor_tensor(cmask[:, cs, :].rearrange("p c (g e) -> p c g e", e=GE),
                                                 choice[:, cs, :].rearrange("p c (g e) -> p c g e", e=GE),
                                                 gmask[:, cs, :].unsqueeze(3).broadcast_to([P, HC, NG, GE]), ALU.mult))

                def chosen_experts():
                    for c in chunks:
                        last = nc.vector.max(ebest[:, c, :], cmask[:, c, :])
                    link(last)
                    for c in chunks:
                        last = nc.vector.match_replace(eleft[:, c, :], ebest[:, c, :], cmask[:, c, :], TAKEN)
                    link(last)

                def chosen_scores():
                    link(nc.vector.scalar_tensor_tensor(out=wsel[:, cs, :], in0=eleft[:, cs, :], scalar=TAKEN,
                                                        in1=score[:, cs, :], op0=ALU.is_equal, op1=ALU.mult))
                    link(nc.vector.tensor_reduce(wsum[:, cs], wsel[:, cs, :], AX.X, ALU.add))

                def weights():
                    link(nc.vector.tensor_scalar(wsum[:, cs], wsum[:, cs], 1e-20, None, ALU.add))
                    link(nc.vector.reciprocal(winv[:, cs], wsum[:, cs]))
                    nc.vector.scalar_tensor_tensor(out=wfin[:, cs, :], in0=wsel[:, cs, :], scalar=ROUTED_SCALING,
                                                   in1=winv[:, cs].unsqueeze(2).broadcast_to([P, HC, E]),
                                                   op0=ALU.mult, op1=ALU.mult).then_inc(wfin_ready, 1)

                return [scores_step, best_of_groups, group_scores, chosen_groups, chosen_experts, chosen_scores,
                        weights]

            def hidden(k):
                _, _, n = chunk_of(k)
                if k == 0:
                    dve.wait_ge(pv_done, NP // 2)
                dve.wait_ge(gate_ready, k + 1)
                dve.wait_ge(u_ready, k + 1)
                if k >= 3:
                    dve.wait_ge(hidl_ready, k - 2)
                routed = n is not None
                dst = gu[:, k % 2, :] if routed else hid[:, k % 3, :]
                nc.vector.tensor_tensor(dst, gu_bank(1, k), gate[:, k % 3, :], ALU.mult).then_inc(gu_ready, 1)
                dve.wait_ge(gu_ready, k + 1)
                if not routed:
                    dve.sem_inc(hid_ready, 1)
                    return
                dve.wait_ge(wb_in[n % WB_RING], 16 * (n // WB_RING + 1))
                nc.vector.tensor_tensor(hid[:, k % 3, :], wb_sb[:, n % WB_RING, :], gu[:, k % 2, :], ALU.mult).then_inc(hid_ready, 1)

            def k_rest_step(i):
                rest_step(i, k_place(i), KSPANS[i], kp, k_high, k_rest, rest_k, 1.0)

            def k_low_step(i):
                low_step(i, KSPANS[i], kp, k_high, k_rest, rest_k, k_low)

            def q_rest_step(i):
                rest_step(i, q_place(i), QSPANS[i], qp, q_high, q_rest, rest_q[:, i % 2, :], QSCALE)

            def q_low_step(i):
                low_step(i, QSPANS[i], qp, q_high, q_rest, rest_q[:, i % 2, :], q_low)

            dve.wait_ge(d_x, 16)
            moments(0, QC, x_sb, stats, mean_var, vareps, var_ready)
            bias_q(0)
            keys_left(0)
            normalise(0)
            k_rest_step(0)
            k_low_step(0)
            dve.wait_ge(d_xrest, 16)
            moments(QC, NC, x_sb, stats, mean_var, vareps, var_ready)
            q_rest_step(0)
            q_low_step(0)
            bias_q(1)
            keys_left(1)
            normalise(1)
            k_rest_step(1)
            k_low_step(1)
            q_rest_step(1)
            q_low_step(1)
            for n in range(PAIRS):
                row_max(n)
            minus_top(0)
            keys_left(2)
            normalise(2)
            k_rest_step(2)
            row_max(PAIRS)
            q_rest_step(2)
            k_low_step(2)
            q_low_step(2)
            keys_left(3)
            normalise(3)
            row_max(PAIRS + 1)
            q_rest_step(3)
            row_max(PAIRS + 2)
            q_low_step(3)
            row_max(PAIRS + 3)
            first_routing = {0: (0, 1), 1: (2, 3), 2: (4,), 4: (5, 6)}
            for n in range(NP):
                b, p = pair_col[n]
                if n + AHEAD < NP:
                    row_max(n + AHEAD)
                    if (n + AHEAD) % PAIRS == PAIRS - 1:
                        minus_top((n + AHEAD) // PAIRS)
                if b >= 1 and p == 1:
                    divide(b - 1, 1)
                if b >= 1 and p == 3:
                    x1_add(b - 1)
                    x1_moments(b - 1)
                if b >= 1 and p == 5:
                    normalise2(b - 1)
                if p == 5:
                    divide(b, 0)
                if b >= 1 and p == 6:
                    xl_step(b - 1)
                if b == B - 1:
                    for i in first_routing.get(p, ()):
                        routing(0)[i]()
            steps = {2: lambda: divide(B - 1, 1), 4: lambda: x1_add(B - 1), 5: lambda: x1_moments(B - 1),
                     6: lambda: normalise2(B - 1), 7: lambda: xl_step(B - 1)}
            steps.update({NI - 8 + n: step for n, step in enumerate(routing(1))})
            for k in range(2 * NI):
                if k in steps:
                    steps[k]()
                hidden(k)


_OUT = "outT"


def kernel(**inputs):
    import ml_dtypes
    import concourse.bacc as bacc
    from concourse.bass_utils import run_bass_kernel_spmd

    a = {k: np.asarray(v) for k, v in inputs.items()}
    bf = ml_dtypes.bfloat16

    def in_turn(w):
        return w.reshape(2, 4, 2, DK, D).transpose(0, 2, 1, 3, 4).reshape(D, D)

    def by_feature(w):
        return in_turn(w).reshape(PAIRS, 2, DK, D).transpose(3, 2, 1, 0).reshape(D, D)

    arrays = {
        "x": a["x"].reshape(T, D),
        "ctxT": a["ctx_1024"].reshape(T, D).T,
        "wqT": by_feature(a["L0_xattn_w_q"]),
        "wkT": by_feature(a["L0_xattn_w_k"]),
        "wvT": in_turn(a["L0_xattn_w_v"]).T,
        "woT": a["L0_xattn_w_o"].T,
        "bo": a["L0_xattn_b_o"],
        "maskq": a["mask_BxSxS2_ik0"],
        "maskT": a["mask_BxSxS2_ik0"].transpose(0, 2, 1),
        "gwT": a["L0_ffn_gate_w"].T,
        "gbias": a["L0_ffn_gate_bias"],
        "wgT": np.concatenate([a["L0_ffn_expert_gate"].reshape(E * I, D), a["L0_ffn_shared_gate"]]).T,
        "wuT": np.concatenate([a["L0_ffn_expert_up"].reshape(E * I, D), a["L0_ffn_shared_up"]]).T,
        "wdT": np.concatenate([a["L0_ffn_expert_down"].transpose(0, 2, 1).reshape(E * I, D),
                               a["L0_ffn_shared_down"].T]),
        "ident": np.eye(P, dtype=np.float32),
        "identb": np.eye(P).astype(bf),
        "ones": np.ones((PARTS, PAIRS * T), bf),
    }
    arrays = {f"in_{k}": np.ascontiguousarray(v) for k, v in arrays.items()}
    nc = bacc.Bacc("TRN2", target_bir_lowering=False, num_devices=1)
    args = [nc.dram_tensor(k, v.shape, mybir.dt.from_np(v.dtype), kind="ExternalInput").ap()
            for k, v in arrays.items()]
    scratch = [nc.dram_tensor("qk_blocks", [BLOCKS, P, 2, T], BF16, kind="Internal").ap(),
               nc.dram_tensor("maxima", [B, PARTS * H, S], BF16, kind="Internal").ap(),
               nc.dram_tensor("routing", [2, E, HALF], F32, kind="Internal").ap()]
    out = nc.dram_tensor(_OUT, [D, T], F32, kind="ExternalOutput").ap()
    build(nc, *args, *scratch, out)
    r = run_bass_kernel_spmd(nc, [arrays], core_ids=[0])
    return r.results[0][_OUT].T.reshape(B, S, D)
```
